# Optimizing a Trainium2 kernel written in Bass

```python
import numpy as np
import jax
import jax.numpy as jnp

def _softmax(x, axis=-1):
    return jax.nn.softmax(x, axis=axis)

def _gelu(x):
    return jax.nn.gelu(x, approximate=True)

def _silu(x):
    return jax.nn.silu(x)

def _sigmoid(x):
    return jax.nn.sigmoid(x)

def _layernorm(x, axis=-1, eps=1e-05):
    m = jnp.mean(x, axis=axis, keepdims=True)
    v = jnp.var(x, axis=axis, keepdims=True)
    return (x - m) / jnp.sqrt(v + eps)

def _scatter_add(tgt, idx, src, axis=0):
    return tgt.at[idx].add(src)

def _segment_sum(src, seg, n):
    return jax.ops.segment_sum(src, seg, n)
kernel_name = 'mk_flamingo_gated_d1_seqx_r8_a310d7'

def setup_inputs(seed: int=0):
    np.random.seed(seed)
    _w = jnp.asarray

    def _rec_inputs():
        import jax
        import jax.numpy as jnp
        _rk = jax.random.key(seed)
        x = -0.0002928 + 1 * jax.random.normal(jax.random.fold_in(_rk, 1), (64, 64, 128), jnp.float32)
        _lenS = 64 - jax.random.randint(jax.random.fold_in(_rk, 7), (64,), 0, max(1, 64 // 4) + 1, jnp.int32)
        _lenS2 = 64 - jax.random.randint(jax.random.fold_in(_rk, 8), (64,), 0, max(1, 64 // 4) + 1, jnp.int32)
        _ctx_1024P = jax.random.normal(jax.random.fold_in(_rk, 11), (64, 16, 128), jnp.float32)
        _ctx_1024c = jax.random.dirichlet(jax.random.fold_in(_rk, 511), 0.3 * jnp.ones((16,), jnp.float32), (64, 64))
        _ctx_1024t = jnp.einsum('bsk,bkd->bsd', _ctx_1024c, _ctx_1024P)
        _ctx_1024t = _ctx_1024t * jax.lax.rsqrt(jnp.mean(jnp.square(_ctx_1024t)) + 1e-12) * 0.953939
        ctx_1024 = -1.39393e-06 + 0.999914 * (_ctx_1024t + 0.3 * jax.random.normal(jax.random.fold_in(_rk, 611), (64, 64, 128), jnp.float32))
        _g = jax.random.normal(jax.random.fold_in(_rk, 9001), (2, 1), jnp.float32)
        _g = jnp.sign(_g) * jnp.maximum(jnp.abs(_g), 1.0) + (_g == 0) * 1.0
        g_xattn = _g[0]
        g_ffn = _g[1]
        return (x, ctx_1024, g_xattn, g_ffn)
    x, ctx_1024, g_xattn, g_ffn = _rec_inputs()

    def _L0_xattn_setup():
        import jax, jax.numpy as jnp
        import numpy as np
        N_HEADS = 16
        KQ_DIM = 64
        EMB_DIM = 128
        CTX_DIM = 128
        EPS = 1e-05

        def _layernorm(x, w, b):
            mu = jnp.mean(x, axis=-1, keepdims=True)
            var = jnp.mean(jnp.square(x - mu), axis=-1, keepdims=True)
            return (x - mu) * jax.lax.rsqrt(var + EPS) * w + b
        key = jax.random.key(seed)
        ks = jax.random.split(key, 10)
        B, SQ, SK = (2, 256, 256)
        inner = N_HEADS * KQ_DIM
        s_e = 1.0 / np.sqrt(EMB_DIM)
        s_c = 1.0 / np.sqrt(CTX_DIM)
        s_i = 1.0 / np.sqrt(inner)
        return {'emb': jax.random.normal(ks[0], (B, SQ, EMB_DIM), jnp.float32), 'context': jax.random.normal(ks[1], (B, SK, CTX_DIM), jnp.float32), 'Wq': jax.random.uniform(ks[2], (inner, EMB_DIM), jnp.float32, -s_e, s_e), 'Wk': jax.random.uniform(ks[3], (inner, CTX_DIM), jnp.float32, -s_c, s_c), 'Wv': jax.random.uniform(ks[4], (inner, CTX_DIM), jnp.float32, -s_c, s_c), 'Wu': jax.random.uniform(ks[5], (EMB_DIM, inner), jnp.float32, -s_i, s_i), 'bu': jax.random.uniform(ks[6], (EMB_DIM,), jnp.float32, -s_i, s_i), 'qn_w': jnp.ones((KQ_DIM,), jnp.float32), 'qn_b': jnp.zeros((KQ_DIM,), jnp.float32), 'kn_w': jnp.ones((KQ_DIM,), jnp.float32), 'kn_b': jnp.zeros((KQ_DIM,), jnp.float32)}
    _L0_xattn_all = _L0_xattn_setup()
    _L0_xattn_in = {k: v for k, v in _L0_xattn_all.items() if k in ('Wq', 'Wk', 'Wv', 'Wu', 'bu', 'qn_w', 'qn_b', 'kn_w', 'kn_b')}
    del _L0_xattn_all

    def _L0_ffn_setup():
        import jax, jax.numpy as jnp
        import numpy as np
        B, S, H = (2, 256, 128)
        F = 512
        E = 8
        TOP_K = 2
        SHARED_SCALE = 0.1
        EPS = 1e-09

        def _moe_forward(x3, Wg, W1, b1, W2, b2, Ws1, bs1, Ws2, bs2):
            b, s, h = x3.shape
            x = x3.reshape(-1, h)
            T = x.shape[0]
            logits = x @ Wg
            probs = jax.nn.softmax(logits, axis=-1)
            vals, idx = jax.lax.top_k(probs, TOP_K)
            weights = vals / (jnp.sum(vals, axis=-1, keepdims=True) + EPS)
            cw = jnp.zeros((T, E), dtype=x.dtype).at[jnp.arange(T)[:, None], idx].set(weights)
            hpre = jnp.einsum('th,ehf->tef', x, W1) + b1
            act = jax.nn.silu(hpre)
            y = jnp.einsum('tef,efh->teh', act, W2) + b2
            out = jnp.einsum('te,teh->th', cw, y)
            shared = jax.nn.silu(x @ Ws1 + bs1) @ Ws2 + bs2
            out = out + SHARED_SCALE * shared
            return out.reshape(b, s, h)
        key = jax.random.key(seed)
        ks = jax.random.split(key, 10)
        sc = 0.02
        return {'hidden_states': jax.random.normal(ks[0], (B, S, H), dtype=jnp.float32), 'Wg': jax.random.normal(ks[1], (H, E), dtype=jnp.float32) * sc, 'W1': jax.random.normal(ks[2], (E, H, F), dtype=jnp.float32) * sc, 'b1': jnp.zeros((E, F), dtype=jnp.float32), 'W2': jax.random.normal(ks[3], (E, F, H), dtype=jnp.float32) * sc, 'b2': jnp.zeros((E, H), dtype=jnp.float32), 'Ws1': jax.random.normal(ks[4], (H, F), dtype=jnp.float32) * sc, 'bs1': jnp.zeros((F,), dtype=jnp.float32), 'Ws2': jax.random.normal(ks[5], (F, H), dtype=jnp.float32) * sc, 'bs2': jnp.zeros((H,), dtype=jnp.float32)}
    _L0_ffn_all = _L0_ffn_setup()
    _L0_ffn_in = {k: v for k, v in _L0_ffn_all.items() if k in ('Wg', 'W1', 'b1', 'W2', 'b2', 'Ws1', 'bs1', 'Ws2', 'bs2')}
    del _L0_ffn_all
    return {'x': x, 'ctx_1024': ctx_1024, 'g_xattn': g_xattn, 'g_ffn': g_ffn, 'L0_xattn_Wq': _L0_xattn_in['Wq'], 'L0_xattn_Wk': _L0_xattn_in['Wk'], 'L0_xattn_Wv': _L0_xattn_in['Wv'], 'L0_xattn_Wu': _L0_xattn_in['Wu'], 'L0_xattn_bu': _L0_xattn_in['bu'], 'L0_xattn_qn_w': _L0_xattn_in['qn_w'], 'L0_xattn_qn_b': _L0_xattn_in['qn_b'], 'L0_xattn_kn_w': _L0_xattn_in['kn_w'], 'L0_xattn_kn_b': _L0_xattn_in['kn_b'], 'L0_ffn_Wg': _L0_ffn_in['Wg'], 'L0_ffn_W1': _L0_ffn_in['W1'], 'L0_ffn_b1': _L0_ffn_in['b1'], 'L0_ffn_W2': _L0_ffn_in['W2'], 'L0_ffn_b2': _L0_ffn_in['b2'], 'L0_ffn_Ws1': _L0_ffn_in['Ws1'], 'L0_ffn_bs1': _L0_ffn_in['bs1'], 'L0_ffn_Ws2': _L0_ffn_in['Ws2'], 'L0_ffn_bs2': _L0_ffn_in['bs2']}

def reference(x, ctx_1024, g_xattn, g_ffn, L0_xattn_Wq, L0_xattn_Wk, L0_xattn_Wv, L0_xattn_Wu, L0_xattn_bu, L0_xattn_qn_w, L0_xattn_qn_b, L0_xattn_kn_w, L0_xattn_kn_b, L0_ffn_Wg, L0_ffn_W1, L0_ffn_b1, L0_ffn_W2, L0_ffn_b2, L0_ffn_Ws1, L0_ffn_bs1, L0_ffn_Ws2, L0_ffn_bs2):
    import jax
    import jax.numpy as jnp

    def _L0_xattn_ref(emb, context, Wq, Wk, Wv, Wu, bu, qn_w, qn_b, kn_w, kn_b):
        import jax, jax.numpy as jnp
        import numpy as np
        N_HEADS = 16
        KQ_DIM = 64
        EMB_DIM = 128
        CTX_DIM = 128
        EPS = 1e-05

        def _layernorm(x, w, b):
            mu = jnp.mean(x, axis=-1, keepdims=True)
            var = jnp.mean(jnp.square(x - mu), axis=-1, keepdims=True)
            return (x - mu) * jax.lax.rsqrt(var + EPS) * w + b
        B, SQ, _ = emb.shape
        SK = context.shape[1]
        q = (emb @ Wq.T).reshape(B, SQ, N_HEADS, KQ_DIM).transpose(0, 2, 1, 3)
        k = (context @ Wk.T).reshape(B, SK, N_HEADS, KQ_DIM).transpose(0, 2, 1, 3)
        v = (context @ Wv.T).reshape(B, SK, N_HEADS, KQ_DIM).transpose(0, 2, 1, 3)
        q = _layernorm(q, qn_w, qn_b)
        k = _layernorm(k, kn_w, kn_b)
        scale = 1.0 / jnp.sqrt(jnp.asarray(KQ_DIM, emb.dtype))
        attn = jnp.einsum('bhqd,bhkd->bhqk', q, k) * scale
        attn = jax.nn.softmax(attn, axis=-1)
        out = jnp.einsum('bhqk,bhkd->bhqd', attn, v)
        out = out.transpose(0, 2, 1, 3).reshape(B, SQ, N_HEADS * KQ_DIM)
        return out @ Wu.T + bu

    def _L0_ffn_ref(hidden_states, Wg, W1, b1, W2, b2, Ws1, bs1, Ws2, bs2):
        import jax, jax.numpy as jnp
        import numpy as np
        B, S, H = (2, 256, 128)
        F = 512
        E = 8
        TOP_K = 2
        SHARED_SCALE = 0.1
        EPS = 1e-09

        def _moe_forward(x3, Wg, W1, b1, W2, b2, Ws1, bs1, Ws2, bs2):
            b, s, h = x3.shape
            x = x3.reshape(-1, h)
            T = x.shape[0]
            logits = x @ Wg
            probs = jax.nn.softmax(logits, axis=-1)
            vals, idx = jax.lax.top_k(probs, TOP_K)
            weights = vals / (jnp.sum(vals, axis=-1, keepdims=True) + EPS)
            cw = jnp.zeros((T, E), dtype=x.dtype).at[jnp.arange(T)[:, None], idx].set(weights)
            hpre = jnp.einsum('th,ehf->tef', x, W1) + b1
            act = jax.nn.silu(hpre)
            y = jnp.einsum('tef,efh->teh', act, W2) + b2
            out = jnp.einsum('te,teh->th', cw, y)
            shared = jax.nn.silu(x @ Ws1 + bs1) @ Ws2 + bs2
            out = out + SHARED_SCALE * shared
            return out.reshape(b, s, h)
        return _moe_forward(hidden_states, Wg, W1, b1, W2, b2, Ws1, bs1, Ws2, bs2)
    x = x + jnp.tanh(g_xattn[0]) * _L0_xattn_ref(_layernorm(x, axis=-1), ctx_1024, L0_xattn_Wq, L0_xattn_Wk, L0_xattn_Wv, L0_xattn_Wu, L0_xattn_bu, L0_xattn_qn_w, L0_xattn_qn_b, L0_xattn_kn_w, L0_xattn_kn_b)
    x = x + jnp.tanh(g_ffn[0]) * _L0_ffn_ref(_layernorm(x, axis=-1), L0_ffn_Wg, L0_ffn_W1, L0_ffn_b1, L0_ffn_W2, L0_ffn_b2, L0_ffn_Ws1, L0_ffn_bs1, L0_ffn_Ws2, L0_ffn_bs2)
    return x

_drawn_inputs = setup_inputs


def setup_inputs(seed=0):
    import zlib

    import numpy as np

    out = dict(_drawn_inputs(seed))
    spreads = {'L0_xattn_qn_w': (1.0, 0.6),
     'L0_xattn_qn_b': (0.0, 0.8),
     'L0_xattn_kn_w': (1.0, 0.6),
     'L0_xattn_kn_b': (0.0, 0.8),
     'L0_ffn_b1': (0.0, 0.526),
     'L0_ffn_b2': (0.0, 0.1),
     'L0_ffn_bs1': (0.0, 0.8),
     'L0_ffn_bs2': (0.0, 0.8)}
    factors = {'L0_xattn_bu': 3.384, 'L0_ffn_Ws1': 8.0, 'L0_ffn_Ws2': 8.0}
    for name, (base, spread) in spreads.items():
        noise = np.random.default_rng([zlib.crc32(name.encode()), seed]).standard_normal(out[name].shape)
        drawn = base * np.exp(spread * noise) if base else spread * noise
        out[name] = jnp.asarray(drawn.astype(out[name].dtype))
    for name, factor in factors.items():
        out[name] = (out[name] * factor).astype(out[name].dtype)
    return out
```

```python
import concourse.bass as bass
from concourse import mybir
from contextlib import ExitStack

F32 = mybir.dt.float32
F32R = mybir.dt.float32r
ALU = mybir.AluOpType
ACT = mybir.ActivationFunctionType
AX = mybir.AxisListType

P = 128
B, S, D = 64, 64, 128
HEADS, HD = 16, 64
INNER = HEADS * HD
TOKENS = B * S
TILES = TOKENS // P
PAIRS = HEADS // 2
E, FF = 8, 512
NX = E + 1
CH = FF // P
GT = 4
GROUPS = TILES // GT
GN = GT * P
LN_EPS = 1e-5
TOPK_EPS = 1e-9
SHARED = 0.1


def flamingo_block(nc, x, ctx, g_xattn, g_ffn, wqT, wkT, wvT, wuT, bu, qn_w, qn_b, kn_w, kn_b,
                   wg, w1, b1, w2, b2, ws1, bs1, ws2, bs2, out):
    x_v = x.rearrange("b s d -> (b s) d").rearrange("(t p) d -> p t d", p=P)
    ctx_v = ctx.rearrange("b s d -> (b s) d").rearrange("(t p) d -> p t d", p=P)
    out_v = out.rearrange("b s d -> (b s) d").rearrange("(t p) d -> p t d", p=P)

    with ExitStack() as stack:
        def sb(name, shape, dt=F32):
            return stack.enter_context(nc.sbuf_tensor(name, shape, dt))

        def bank(name):
            return stack.enter_context(nc.psum_tensor(name, [P, 512], F32))

        def sem(name):
            return stack.enter_context(nc.semaphore(name))

        x_res = sb("x_res", [P, TILES, D])
        c_in = sb("c_in", [P, 2, D])
        xn = sb("xn", [P, D])
        xc_hi = sb("xc_hi", [P, 2, 2, P], F32R)
        xc_lo = sb("xc_lo", [P, 2, 2, P], F32R)
        w_raw = sb("w_raw", [P, 3, INNER])
        w_hi = sb("w_hi", [P, 3, INNER], F32R)
        w_lo = sb("w_lo", [P, 3, INNER], F32R)
        w_mean = sb("w_mean", [P, 2, HEADS])
        wu_sb = sb("wu_sb", [P, PAIRS, D])
        wide = sb("wide", [P, 4, INNER])
        sq = wide[:, 0:2, :]
        ss = sb("ss", [P, 2, HEADS])
        rstd = sb("rstd", [P, 2, HEADS])
        var_eps = sb("var_eps", [P, 2, HEADS])
        qk_n = wide[:, 2:4, :]
        qk_T = sb("qk_T", [P, 2, PAIRS, P])
        v_sb = sb("v_sb", [P, 2, INNER])
        prob = sb("prob", [P, PAIRS, 2, S])
        prob_T = sb("prob_T", [P, PAIRS, P])
        o_T = sb("o_T", [P, PAIRS, 2, S])
        mx = sb("mx", [P, 2, PAIRS])
        sm = sb("sm", [P, PAIRS * 2])
        rinv = sb("rinv", [P, PAIRS * 2])
        y_tmp = sb("y_tmp", [P, D])
        lnw = sb("lnw", [P, 4])
        gates = sb("gates", [P, 2])
        tg = sb("tg", [P, 2])
        bu_b = sb("bu_b", [P, D])
        tgbu = sb("tgbu", [P, D])
        ident = sb("ident", [P, P])
        expo = sb("expo", [P, 2, HEADS])
        eps = sb("eps", [P, 2, HEADS])
        bn6 = sb("bn6", [P, 6])
        mv = sb("mv", [P, 2])
        xv_eps = sb("xv_eps", [P, 1])
        x_rstd = sb("x_rstd", [P, 1])
        wg_raw = sb("wg_raw", [P, E])
        wg_hi = sb("wg_hi", [P, E], F32R)
        wg_lo = sb("wg_lo", [P, E], F32R)
        w1_raw = sb("w1_raw", [P, NX, FF])
        w1_hi = sb("w1_hi", [P, NX, FF], F32R)
        w1_lo = sb("w1_lo", [P, NX, FF], F32R)
        w2_sb = sb("w2_sb", [P, NX, CH, D])
        b1_sb = sb("b1_sb", [P, NX, CH])
        b2_sb = sb("b2_sb", [NX, D])
        gT_hi = sb("gT_hi", [P, GN], F32R)
        gT_lo = sb("gT_lo", [P, GN], F32R)
        gxn = sb("gxn", [P, GT, D])
        act = wide[:, :, :].rearrange("p a n -> p (a n)").rearrange("p (a c n) -> p a c n", a=2, c=CH)
        acc = sb("acc", [P, GT, D])
        cw = sb("cw", [P, GT, NX])
        cwT = sb("cwT", [NX, GN])
        gb6 = sb("gb6", [P, GT, 6])
        gmv = sb("gmv", [P, GT, 2])
        gve = sb("gve", [P, GT])
        grs = sb("grs", [P, GT])
        gl = sb("gl", [P, GT, E])
        gp = sb("gp", [P, GT, E])
        gm = sb("gm", [P, GT])
        gs = sb("gs", [P, GT])
        gtop = sb("gtop", [P, GT, 8])
        gidx = sb("gidx", [P, GT, 8], mybir.dt.uint32)
        gidf = sb("gidf", [P, GT, 2])
        gw = sb("gw", [P, GT, 2])
        goh = sb("goh", [P, 2, GT, E])
        iot = sb("iot", [P, E])
        iot_i = sb("iot_i", [P, E], mybir.dt.int32)
        outb = sb("outb", [P, GT, D])

        ps = [bank(f"ps{i}") for i in range(8)]

        const_in, wq_in, wu_in, ffw_in = sem("const_in"), sem("wq_in"), sem("wu_in"), sem("ffw_in")
        x_in = sem("x_in")
        c_loaded = [sem("c_loaded0"), sem("c_loaded1")]
        ones_ready, ident_ready, expo_ready = sem("ones_ready"), sem("ident_ready"), sem("expo_ready")
        wprep, w_ready, tanh_ready, tgbu_ready = sem("wprep"), sem("w_ready"), sem("tanh_ready"), sem("tgbu_ready")
        bn_done, mv_ready, xve_ready, xrs_ready, xn_ready = (sem(n) for n in ("bn_done", "mv_ready", "xve_ready", "xrs_ready", "xn_ready"))
        xt_done, xhi_ready, xlo_ready = sem("xt_done"), sem("xhi_ready"), sem("xlo_ready")
        proj_done, sq_ready, ss_ready, ve_ready, rstd_ready, qn_ready = (
            sem(n) for n in ("proj_done", "sq_ready", "ss_ready", "ve_ready", "rstd_ready", "qn_ready"))
        qt_done, kt_done, qT_ready, kT_ready = sem("qt_done"), sem("kt_done"), sem("qT_ready"), sem("kT_ready")
        v_done, v_ready = sem("v_done"), sem("v_ready")
        s_done, mx_ready, sub_ready, exp_ready, sum_ready, rinv_ready, p_ready = (
            sem(n) for n in ("s_done", "mx_ready", "sub_ready", "exp_ready", "sum_ready", "rinv_ready", "p_ready"))
        pt_done, pt0_ready, pt1_ready = sem("pt_done"), sem("pt0_ready"), sem("pt1_ready")
        o_done, o_ready, y_done, y_read, x1_ready = (sem(n) for n in ("o_done", "o_ready", "y_done", "y_read", "x1_ready"))
        f_bn, f_mv, f_ve, f_rs, f_xn = (sem(n) for n in ("f_bn", "f_mv", "f_ve", "f_rs", "f_xn"))
        f_t, f_hi, f_lo, f_lg, f_dve, f_exp, f_cw, f_ct, f_cT, f_ab, f_acc0 = (
            sem(n) for n in ("f_t", "f_hi", "f_lo", "f_lg", "f_dve", "f_exp", "f_cw", "f_ct", "f_cT", "f_ab", "f_acc0"))
        f_bias, h_done, act_ready, fy_done, fy_read, f_out, f_stored, ffw_ready = (
            sem(n) for n in ("f_bias", "h_done", "act_ready", "fy_done", "fy_read", "f_out", "f_stored", "ffw_ready"))

        block = stack.enter_context(nc.Block())

        STEADY = range(2, TILES - 2)

        def steps(eng, step):
            for s in range(-2, STEADY.start):
                step(s, s % 2, s)
            with eng.Fori(0, len(STEADY) // 2) as i:
                for half in range(2):
                    step(2 * i + (STEADY.start + half), half, STEADY.start)
            for s in range(STEADY.stop, TILES + 1):
                step(s, s % 2, s)

        def wait_apart(eng, semaphore, value):
            if not isinstance(value, int):
                eng.compute_val(value)
            eng.wait_ge(ident_ready, 1)
            eng.wait_ge(semaphore, value)

        def has(s):
            return 0 <= s < TILES

        @block.sync
        def _(sp):
            for c in range(4):
                n = TILES // 4
                sp.dma_start(x_res[:, c * n:(c + 1) * n, :], x_v[:, c * n:(c + 1) * n, :]).then_inc(x_in, 16)
                if c == 0:
                    for t in range(2):
                        sp.dma_start(c_in[:, t, :], ctx_v[:, t, :]).then_inc(c_loaded[t], 16)
                    for n_, w in enumerate((wqT, wkT, wvT)):
                        sp.dma_start(w_raw[:, n_, :], w).then_inc(wq_in, 16)
            sp.dma_start(wu_sb[:, :, :], wuT.rearrange("(c p) n -> p c n", p=P)).then_inc(wu_in, 16)
            sp.dma_start(wg_raw[:, :], wg).then_inc(ffw_in, 16)
            sp.dma_start(w1_raw[:, 0:E, :], w1.rearrange("e h f -> h e f")).then_inc(ffw_in, 16)
            sp.dma_start(w1_raw[:, E, :], ws1).then_inc(ffw_in, 16)
            sp.dma_start(w2_sb[:, 0:E, :, :].rearrange("p e c n -> p (e c) n"),
                         w2.rearrange("e f h -> (e f) h").rearrange("(k p) n -> p k n", p=P)).then_inc(ffw_in, 16)
            sp.dma_start(w2_sb[:, E, :, :], ws2.rearrange("(c p) n -> p c n", p=P)).then_inc(ffw_in, 16)
            sp.dma_start(b1_sb[:, 0:E, :].rearrange("p e c -> p (e c)"), b1).then_inc(ffw_in, 16)
            sp.dma_start(b1_sb[:, E, :], bs1).then_inc(ffw_in, 16)
            sp.dma_start(b2_sb[0:E, :], b2).then_inc(ffw_in, 16)
            sp.dma_start(b2_sb[E:NX, :], bs2.rearrange("(a n) -> a n", a=1)).then_inc(ffw_in, 16)
            with sp.Fori(0, TILES // 2 - 1) as i:
                for half in range(2):
                    sp.compute_val(2 * i + (half + 2))
                    wait_apart(sp, xt_done, 2 * i + (half + 1))
                    sp.dma_start(c_in[:, half, :], ctx_v[:, bass.ds(2 * i + (half + 2), 1), :].rearrange("p a d -> p (a d)")
                                 ).then_inc(c_loaded[half], 16)
            with sp.Fori(0, GROUPS) as g:
                sp.wait_ge(f_out, g + 1)
                sp.dma_start(out_v[:, bass.ds(GT * g, GT), :], outb[:, :, :]).then_inc(f_stored, 16)
            sp.wait_ge(f_stored, 16 * GROUPS + 16)

        @block.scalar
        def _(sc):
            for n, src in enumerate((g_xattn, g_ffn)):
                sc.dma_start(gates[:, n:n + 1], src.rearrange("(a n) -> a n", a=1).partition_broadcast(P).rearrange("p a n -> p (a n)")).then_inc(const_in, 16)
            sc.dma_start(bu_b[:, :], bu.rearrange("(a n) -> a n", a=1).partition_broadcast(P).rearrange("p a n -> p (a n)")).then_inc(const_in, 16)
            for n, src in enumerate((qn_w, qn_b, kn_w, kn_b)):
                for h in range(2):
                    sc.dma_start(lnw[h * HD:(h + 1) * HD, n:n + 1], src.rearrange("(p a) -> p a", a=1)).then_inc(const_in, 16)
            sc.wait_ge(const_in, 11 * 16)
            nc.scalar.activation(tg[:, :], gates[:, :], ACT.Tanh).then_inc(tanh_ready, 1)

            def step(s, par, k):
                if has(k):
                    for j in range(2):
                        sc.wait_ge(qt_done, 2 * s + (j + 1))
                        nc.scalar.activation(qk_T[:, 0, 4 * j:4 * j + 4, :].rearrange("p a n -> p (a n)"), ps[6 + j][:, :],
                                             ACT.Identity, bias=lnw[:, 1:2], scale=lnw[:, 0:1]).then_inc(qT_ready, 1)
                if has(k + 1):
                    if k + 1 >= 1:
                        sc.wait_ge(ss_ready, 2 * s + 2)
                    for j in range(4):
                        sc.wait_ge(proj_done, 4 * s + (5 + j))
                        nc.scalar.activation(sq[:, j // 2, (j % 2) * 512:(j % 2) * 512 + 512], ps[j][:, :],
                                             ACT.Square, scale=HD ** -0.5).then_inc(sq_ready, 1)
                if has(k):
                    if k >= 2:
                        sc.wait_ge(o_done, 2 * s - 2)
                    for j in range(2):
                        sc.wait_ge(v_done, 2 * s + (j + 1))
                        nc.scalar.activation(v_sb[:, par, j * 512:(j + 1) * 512], ps[4 + j][:, :], ACT.Copy).then_inc(v_ready, 1)
                if has(k - 1):
                    sc.wait_ge(pt_done, 2 * s - 1)
                    nc.scalar.activation(prob_T[:, 0:4, :].rearrange("p a n -> p (a n)"), ps[6][:, :], ACT.Copy).then_inc(pt0_ready, 1)
                if has(k):
                    sc.wait_ge(sub_ready, 2 * s + 2)
                    p_all = prob[:, :, :, :].rearrange("p a b n -> p (a b n)")
                    nc.scalar.activation(p_all, p_all, ACT.Exp, scale=HD ** -0.5).then_inc(exp_ready, 1)
                if has(k - 1):
                    if k >= 2:
                        sc.wait_ge(y_done, s - 1)
                    for j in range(2):
                        sc.wait_ge(o_done, 2 * s + (j - 1))
                        nc.scalar.activation(o_T[:, :, j, :], ps[6 + j][:, :].rearrange("p (a n) -> p a n", a=PAIRS),
                                             ACT.Copy).then_inc(o_ready, 1)
                if has(k + 2):
                    sc.wait_ge(xt_done, s + 3)
                    nc.scalar.activation(xc_hi[:, par, :, :].rearrange("p a n -> p (a n)"), ps[6][:, 0:256], ACT.Copy).then_inc(xhi_ready, 1)

            steps(sc, step)

            with sc.Fori(0, GROUPS) as g:
                sc.wait_ge(f_t, g + 1)
                nc.scalar.activation(gT_hi[:, :], ps[6][:, :], ACT.Copy).then_inc(f_hi, 1)
                sc.wait_ge(f_dve, 10 * g + 2)
                nc.scalar.activation(gp[:, :, :], gp[:, :, :], ACT.Exp).then_inc(f_exp, 1)
                for e in range(NX):
                    for c in range(CH):
                        sc.wait_ge(h_done, NX * CH * g + (e * CH + c + 1))
                        if c == 0 and e >= 2:
                            sc.wait_ge(fy_done, NX * g + (e - 1))
                        nc.scalar.activation(act[:, e % 2, c, :], ps[c][:, :], ACT.Silu,
                                             bias=b1_sb[:, (e + E) % NX, c:c + 1]).then_inc(act_ready, 1)
                sc.wait_ge(fy_done, NX * g + NX)

        @block.gpsimd
        def _(gp_):
            nc.gpsimd.memset(ident[:, :], 0.0).then_inc(ones_ready, 1)
            gp_.wait_ge(ones_ready, 1)
            nc.gpsimd.affine_select(out=ident[:, :], in_=ident[:, :], compare_op=ALU.not_equal, fill=1.0,
                                    base=0, pattern=[[-1, P]], channel_multiplier=1).then_inc(ident_ready, 1)
            nc.gpsimd.memset(expo[:, :, :], -0.5).then_inc(expo_ready, 1)
            nc.gpsimd.memset(eps[:, :, :], LN_EPS).then_inc(expo_ready, 1)
            nc.gpsimd.iota(iot_i[:, :], pattern=[[1, E]], base=0, channel_multiplier=0).then_inc(expo_ready, 1)
            gp_.wait_ge(expo_ready, 3)
            nc.gpsimd.tensor_copy(iot[:, :], iot_i[:, :]).then_inc(expo_ready, 1)

            def step(s, par, k):
                if has(k + 2):
                    gp_.wait_ge(mv_ready, s + 3)
                    nc.gpsimd.tensor_tensor(xv_eps[:, :], mv[:, 1:2], eps[:, 0, 0:1], ALU.add).then_inc(xve_ready, 1)
                    gp_.wait_ge(xve_ready, s + 3)
                    nc.gpsimd.tensor_tensor(x_rstd[:, :], xv_eps[:, :], expo[:, 0, 0:1], ALU.pow).then_inc(xrs_ready, 1)
                if has(k + 1):
                    for n in range(2):
                        gp_.wait_ge(ss_ready, 2 * s + (3 + n))
                        nc.gpsimd.tensor_tensor(var_eps[:, n, :], ss[:, n, :], eps[:, n, :], ALU.add).then_inc(ve_ready, 1)
                        gp_.wait_ge(ve_ready, 2 * s + (3 + n))
                        nc.gpsimd.tensor_tensor(rstd[:, n, :], var_eps[:, n, :], expo[:, n, :], ALU.pow).then_inc(rstd_ready, 1)
                if has(k):
                    gp_.wait_ge(rinv_ready, s + 1)
                    pv = prob[:, :, :, :].rearrange("p a b n -> p (a b) n")
                    nc.gpsimd.tensor_tensor(pv, pv, rinv[:, :].unsqueeze(2).to_broadcast([P, 2 * PAIRS, S]), ALU.mult).then_inc(p_ready, 1)

            steps(gp_, step)

            gp_.wait_ge(ffw_in, 9 * 16)
            nc.gpsimd.tensor_copy(w1_hi[:, :, :], w1_raw[:, :, :]).then_inc(ffw_ready, 1)
            nc.gpsimd.tensor_copy(wg_hi[:, :], wg_raw[:, :]).then_inc(ffw_ready, 1)
            gp_.wait_ge(ffw_ready, 2)
            nc.gpsimd.tensor_tensor(w1_lo[:, :, :], w1_raw[:, :, :], w1_hi[:, :, :].bitcast(F32), ALU.subtract).then_inc(ffw_ready, 1)
            nc.gpsimd.tensor_tensor(wg_lo[:, :], wg_raw[:, :], wg_hi[:, :].bitcast(F32), ALU.subtract).then_inc(ffw_ready, 1)
            with gp_.Fori(0, GROUPS) as g:
                gp_.wait_ge(f_mv, GT * g + GT)
                nc.gpsimd.tensor_tensor(gve[:, :], gmv[:, :, 1], eps[:, 0, 0:GT], ALU.add).then_inc(f_ve, 1)
                gp_.wait_ge(f_ve, g + 1)
                nc.gpsimd.tensor_tensor(grs[:, :], gve[:, :], expo[:, 0, 0:GT], ALU.pow).then_inc(f_rs, 1)

        @block.vector
        def _(ve):
            ve.wait_ge(wq_in, 48)
            for n in range(2):
                nc.vector.tensor_reduce(w_mean[:, n, :], w_raw[:, n, :].rearrange("p (h d) -> p h d", h=HEADS), AX.X, ALU.add).then_inc(wprep, 1)
            ve.wait_ge(wprep, 2)
            nc.vector.tensor_scalar(w_mean[:, :, :], w_mean[:, :, :], 1.0 / HD, None, ALU.mult).then_inc(wprep, 1)
            ve.wait_ge(wprep, 3)
            for n in range(2):
                wv_ = w_raw[:, n, :].rearrange("p (h d) -> p h d", h=HEADS)
                nc.vector.tensor_tensor(wv_, wv_, w_mean[:, n, :].unsqueeze(2).to_broadcast([P, HEADS, HD]), ALU.subtract).then_inc(wprep, 1)
            ve.wait_ge(wprep, 5)
            nc.vector.tensor_copy(w_hi[:, :, :], w_raw[:, :, :]).then_inc(wprep, 1)
            ve.wait_ge(wprep, 6)
            nc.vector.tensor_tensor(w_lo[:, :, :], w_raw[:, :, :], w_hi[:, :, :].bitcast(F32), ALU.subtract).then_inc(w_ready, 1)
            ve.wait_ge(tanh_ready, 1)
            nc.vector.tensor_scalar(tgbu[:, :], bu_b[:, :], tg[:, 0:1], None, ALU.mult).then_inc(tgbu_ready, 1)
            ve.wait_ge(x_in, 64)

            def step(s, par, k):
                if has(k + 2):
                    if k + 2 >= 1:
                        ve.wait_ge(xn_ready, s + 2)
                    xt = x_res[:, s + 2, :] if isinstance(s, int) else x_res[:, bass.ds(s + 2, 1), :].rearrange("p a d -> p (a d)")
                    nc.vector.bn_stats(bn6[:, :], xt).then_inc(bn_done, 1)
                    wait_apart(ve, bn_done, s + 3)
                    nc.vector.bn_aggr(mv[:, :], bn6[:, :]).then_inc(mv_ready, 1)
                if has(k):
                    for j in range(2):
                        ve.wait_ge(kt_done, 2 * s + (j + 1))
                        nc.vector.tensor_scalar(qk_T[:, 1, 4 * j:4 * j + 4, :].rearrange("p a n -> p (a n)"), ps[6 + j][:, :],
                                                lnw[:, 2:3], lnw[:, 3:4], ALU.mult, ALU.add).then_inc(kT_ready, 1)
                if has(k + 2):
                    ve.wait_ge(xrs_ready, s + 3)
                    if k + 2 >= 1:
                        ve.wait_ge(xt_done, s + 2)
                    nc.vector.tensor_scalar(xn[:, :], xt, mv[:, 0:1], x_rstd[:, 0:1], ALU.subtract, ALU.mult).then_inc(xn_ready, 1)
                if has(k + 1):
                    for n in range(2):
                        ve.wait_ge(sq_ready, 4 * s + (6 + 2 * n))
                        if k + 1 >= 1:
                            ve.wait_ge(ve_ready, 2 * s + (1 + n))
                        nc.vector.tensor_reduce(ss[:, n, :], sq[:, n, :].rearrange("p (h d) -> p h d", h=HEADS), AX.X, ALU.add).then_inc(ss_ready, 1)
                if has(k - 1):
                    ve.wait_ge(pt_done, 2 * s)
                    nc.vector.tensor_copy(prob_T[:, 4:8, :].rearrange("p a n -> p (a n)"), ps[7][:, :]).then_inc(pt1_ready, 1)
                if has(k + 1):
                    for j in range(4):
                        n, half = j // 2, j % 2
                        ve.wait_ge(rstd_ready, 2 * s + (3 + n))
                        if k >= 0:
                            ve.wait_ge(kt_done, 2 * s + 2)
                        nc.vector.tensor_tensor(
                            qk_n[:, n, half * 512:(half + 1) * 512].rearrange("p (h d) -> p h d", h=8),
                            ps[j][:, :].rearrange("p (h d) -> p h d", h=8),
                            rstd[:, n, half * 8:half * 8 + 8].unsqueeze(2).to_broadcast([P, 8, HD]), ALU.mult).then_inc(qn_ready, 1)
                if has(k):
                    if k >= 1:
                        ve.wait_ge(pt_done, 2 * s)
                    for j in range(2):
                        ve.wait_ge(s_done, 2 * s + (j + 1))
                        sv = ps[4 + j][:, :].rearrange("p (a n) -> p a n", a=PAIRS)
                        nc.vector.tensor_reduce(mx[:, j, :], sv, AX.X, ALU.max).then_inc(mx_ready, 1)
                        ve.wait_ge(mx_ready, 2 * s + (j + 1))
                        nc.vector.tensor_tensor(prob[:, :, j, :], sv, mx[:, j, :].unsqueeze(2).to_broadcast([P, PAIRS, S]),
                                                ALU.subtract).then_inc(sub_ready, 1)
                    ve.wait_ge(exp_ready, s + 1)
                    nc.vector.tensor_reduce(sm[:, :], prob[:, :, :, :].rearrange("p a b n -> p (a b) n"), AX.X, ALU.add).then_inc(sum_ready, 1)
                    ve.wait_ge(sum_ready, s + 1)
                    if k >= 1:
                        ve.wait_ge(p_ready, s)
                    nc.vector.reciprocal(rinv[:, :], sm[:, :]).then_inc(rinv_ready, 1)
                if has(k + 2):
                    ve.wait_ge(xhi_ready, s + 3)
                    nc.vector.tensor_tensor(xc_lo[:, par, :, :].rearrange("p a n -> p (a n)"), ps[6][:, 0:256],
                                            xc_hi[:, par, :, :].rearrange("p a n -> p (a n)").bitcast(F32), ALU.subtract).then_inc(xlo_ready, 1)
                if has(k - 1):
                    ve.wait_ge(y_done, s)
                    xs = x_res[:, s - 1, :] if isinstance(s, int) else x_res[:, bass.ds(s - 1, 1), :].rearrange("p a d -> p (a d)")
                    if k >= 2:
                        ve.wait_ge(x1_ready, s - 1)
                    nc.vector.scalar_tensor_tensor(y_tmp[:, :], ps[7][:, 0:D], tg[:, 0:1], tgbu[:, :], ALU.mult, ALU.add).then_inc(y_read, 1)
                    ve.wait_ge(y_read, s)
                    nc.vector.tensor_tensor(xs, xs, y_tmp[:, :], ALU.add).then_inc(x1_ready, 1)

            ve.wait_ge(tgbu_ready, 1)
            steps(ve, step)
            ve.wait_ge(x1_ready, TILES)
            nc.vector.memset(cw[:, :, E:NX], SHARED).then_inc(f_cw, 1)
            nc.vector.memset(outb[:, :, :], 0.0).then_inc(f_stored, 16)
            ve.wait_ge(f_stored, 16)

            with ve.Fori(0, GROUPS) as g:
                for j in range(GT):
                    xt = x_res[:, bass.ds(GT * g + j, 1), :].rearrange("p a d -> p (a d)")
                    nc.vector.bn_stats(gb6[:, j, :], xt).then_inc(f_bn, 1)
                for j in range(GT):
                    wait_apart(ve, f_bn, GT * g + (j + 1))
                    nc.vector.bn_aggr(gmv[:, j, :], gb6[:, j, :]).then_inc(f_mv, 1)
                ve.wait_ge(f_rs, g + 1)
                for j in range(GT):
                    xt = x_res[:, bass.ds(GT * g + j, 1), :].rearrange("p a d -> p (a d)")
                    nc.vector.tensor_scalar(gxn[:, j, :], xt, gmv[:, j, 0:1], grs[:, j:j + 1], ALU.subtract, ALU.mult).then_inc(f_xn, 1)
                ve.wait_ge(f_hi, g + 1)
                nc.vector.tensor_tensor(gT_lo[:, :], ps[6][:, :], gT_hi[:, :].bitcast(F32), ALU.subtract).then_inc(f_lo, 1)
                ve.wait_ge(f_lg, g + 1)
                lg = ps[7][:, 0:GT * E].rearrange("p (j e) -> p j e", j=GT)
                nc.vector.tensor_reduce(gm[:, :], lg, AX.X, ALU.max).then_inc(f_dve, 1)
                ve.wait_ge(f_dve, 10 * g + 1)
                nc.vector.tensor_tensor(gp[:, :, :], lg, gm[:, :].unsqueeze(2).to_broadcast([P, GT, E]), ALU.subtract).then_inc(f_dve, 1)
                ve.wait_ge(f_exp, g + 1)
                nc.vector.tensor_reduce(gs[:, :], gp[:, :, :], AX.X, ALU.add).then_inc(f_dve, 1)
                ve.wait_ge(f_dve, 10 * g + 3)
                nc.vector.reciprocal(gs[:, :], gs[:, :]).then_inc(f_dve, 1)
                ve.wait_ge(f_dve, 10 * g + 4)
                nc.vector.tensor_tensor(gp[:, :, :], gp[:, :, :], gs[:, :].unsqueeze(2).to_broadcast([P, GT, E]), ALU.mult).then_inc(f_dve, 1)
                wait_apart(ve, f_dve, 10 * g + 5)
                for j in range(GT):
                    nc.vector.max(gtop[:, j, :], gp[:, j, :]).then_inc(f_ab, 1)
                wait_apart(ve, f_ab, 2 * GT * g + GT)
                for j in range(GT):
                    nc.vector.max_index(gidx[:, j, :], gtop[:, j, :], gp[:, j, :]).then_inc(f_ab, 1)
                nc.vector.tensor_reduce(gs[:, :], gtop[:, :, 0:2], AX.X, ALU.add).then_inc(f_dve, 1)
                ve.wait_ge(f_dve, 10 * g + 6)
                nc.vector.tensor_scalar(gs[:, :], gs[:, :], TOPK_EPS, None, ALU.add).then_inc(f_dve, 1)
                ve.wait_ge(f_dve, 10 * g + 7)
                nc.vector.reciprocal(gs[:, :], gs[:, :]).then_inc(f_dve, 1)
                ve.wait_ge(f_dve, 10 * g + 8)
                nc.vector.tensor_tensor(gw[:, :, :], gtop[:, :, 0:2], gs[:, :].unsqueeze(2).to_broadcast([P, GT, 2]), ALU.mult).then_inc(f_dve, 1)
                ve.wait_ge(f_ab, 2 * GT * g + 2 * GT)
                nc.vector.tensor_copy(gidf[:, :, :], gidx[:, :, 0:2]).then_inc(f_dve, 1)
                ve.wait_ge(f_dve, 10 * g + 10)
                for n in range(2):
                    nc.vector.tensor_tensor(goh[:, n, :, :], iot[:, :].unsqueeze(1).to_broadcast([P, GT, E]),
                                            gidf[:, :, n].unsqueeze(2).to_broadcast([P, GT, E]), ALU.is_equal).then_inc(f_acc0, 1)
                ve.wait_ge(f_acc0, 5 * g + 2)
                for n in range(2):
                    nc.vector.tensor_tensor(goh[:, n, :, :], goh[:, n, :, :],
                                            gw[:, :, n].unsqueeze(2).to_broadcast([P, GT, E]), ALU.mult).then_inc(f_acc0, 1)
                ve.wait_ge(f_acc0, 5 * g + 4)
                nc.vector.tensor_tensor(cw[:, :, 0:E], goh[:, 0, :, :], goh[:, 1, :, :], ALU.add).then_inc(f_cw, 1)
                ve.wait_ge(f_ct, g + 1)
                nc.vector.tensor_copy(cwT[:, :], ps[6][0:NX, :]).then_inc(f_cT, 1)
                ve.wait_ge(f_bias, g + 1)
                nc.vector.tensor_copy(acc[:, :, :].rearrange("p j d -> p (j d)"), ps[7][:, :]).then_inc(f_acc0, 1)
                ve.wait_ge(f_acc0, 5 * g + 5)
                for e in range(NX):
                    ve.wait_ge(fy_done, NX * g + (e + 1))
                    for j in range(GT):
                        w = (e + E) % NX
                        if e > 0:
                            ve.wait_ge(fy_read, GT * NX * g + (GT * (e - 1) + j + 1))
                        nc.vector.scalar_tensor_tensor(acc[:, j, :], ps[4 + e % 2][:, j * D:(j + 1) * D], cw[:, j, w:w + 1],
                                                       acc[:, j, :], ALU.mult, ALU.add).then_inc(fy_read, 1)
                ve.wait_ge(fy_read, GT * NX * g + GT * NX)
                ve.wait_ge(f_stored, 16 * g + 16)
                nc.vector.scalar_tensor_tensor(outb[:, :, :].rearrange("p j d -> p (j d)"), acc[:, :, :].rearrange("p j d -> p (j d)"),
                                               tg[:, 1:2], x_res[:, bass.ds(GT * g, GT), :].rearrange("p j d -> p (j d)"),
                                               ALU.mult, ALU.add).then_inc(f_out, 1)

        @block.tensor
        def _(pe):
            pe.wait_ge(ident_ready, 1)
            pe.wait_ge(w_ready, 1)
            pe.wait_ge(wu_in, 16)

            def project(out_bank, par, src, w, cols):
                nc.tensor.matmul(out_bank, xc_hi[:, par, src, :], w_hi[:, w, cols], start=True, stop=False)
                nc.tensor.matmul(out_bank, xc_hi[:, par, src, :], w_lo[:, w, cols], start=False, stop=False)
                return nc.tensor.matmul(out_bank, xc_lo[:, par, src, :], w_hi[:, w, cols], start=False, stop=True)

            def step(s, par, k):
                cols = (slice(0, 512), slice(512, 1024))
                if has(k):
                    pe.wait_ge(qn_ready, 4 * s + 4)
                    if has(k + 1):
                        pe.wait_ge(xlo_ready, s + 2)
                    if k >= 2:
                        pe.wait_ge(o_ready, 2 * s - 2)
                        pe.wait_ge(y_read, s - 1)
                    for n, (done, free) in enumerate(((qt_done, None), (kt_done, qT_ready))):
                        for j in range(2):
                            if free is not None:
                                pe.wait_ge(free, 2 * s + (j + 1))
                            for a in range(4):
                                c0 = (4 * j + a) * P
                                last = nc.tensor.transpose(ps[6 + j][:, a * P:(a + 1) * P], qk_n[:, n, c0:c0 + P], ident[:, :])
                            last.then_inc(done, 1)
                if has(k + 1):
                    if not has(k):
                        pe.wait_ge(xlo_ready, s + 2)
                    opar = 1 - par
                    for j in range(4):
                        project(ps[j][:, :], opar, j // 2, j // 2, cols[j % 2]).then_inc(proj_done, 1)
                if has(k):
                    if k >= 1:
                        pe.wait_ge(sub_ready, 2 * s)
                    for j in range(2):
                        project(ps[4 + j][:, :], par, 1, 2, cols[j]).then_inc(v_done, 1)
                if has(k - 1):
                    pe.wait_ge(p_ready, s)
                    for j in range(2):
                        if has(k):
                            pe.wait_ge(kT_ready, 2 * s + (j + 1))
                        elif j == 0:
                            pe.wait_ge(o_ready, 2 * s - 2)
                            pe.wait_ge(y_read, s - 1)
                        for a in range(4):
                            last = nc.tensor.transpose(ps[6 + j][:, a * P:(a + 1) * P],
                                                       prob[:, 4 * j + a, :, :].rearrange("p b n -> p (b n)"), ident[:, :])
                        last.then_inc(pt_done, 1)
                if has(k):
                    wait_apart(pe, kT_ready, 2 * s + 2)
                    pe.wait_ge(qT_ready, 2 * s + 2)
                    for b in range(2):
                        wait_apart(pe, v_ready, 2 * s + (b + 1))
                        for p in range(PAIRS):
                            for h in range(2):
                                rows = slice(h * HD, (h + 1) * HD)
                                last = nc.tensor.matmul(ps[4 + b][rows, p * S:(p + 1) * S], qk_T[rows, 0, p, b * S:(b + 1) * S],
                                                        qk_T[rows, 1, p, b * S:(b + 1) * S], start=True, stop=True)
                        last.then_inc(s_done, 1)
                if has(k - 1):
                    wait_apart(pe, pt0_ready, s)
                    pe.wait_ge(pt1_ready, s)
                    vpar = 1 - par
                    for b in range(2):
                        rows = slice(b * S, (b + 1) * S)
                        for p in range(PAIRS):
                            for h in range(2):
                                last = nc.tensor.matmul(ps[6 + b][h * HD:(h + 1) * HD, p * S:(p + 1) * S],
                                                        v_sb[rows, vpar, (2 * p + h) * HD:(2 * p + h + 1) * HD],
                                                        prob_T[rows, p, h * S:(h + 1) * S], start=True, stop=True)
                        last.then_inc(o_done, 1)
                if has(k + 2):
                    pe.wait_ge(xn_ready, s + 3)
                    pe.wait_ge(c_loaded[par], 8 * (s + 2 - par) + 16)
                    if has(k - 1):
                        pe.wait_ge(o_ready, 2 * s - 1)
                    elif has(k):
                        pe.wait_ge(kT_ready, 2 * s + 2)
                    elif has(k + 1):
                        pe.wait_ge(xlo_ready, s + 2)
                    nc.tensor.transpose(ps[6][:, 0:P], xn[:, :], ident[:, :])
                    nc.tensor.transpose(ps[6][:, P:2 * P], c_in[:, par, :], ident[:, :]).then_inc(xt_done, 1)
                if has(k - 1):
                    pe.wait_ge(o_ready, 2 * s)
                    for p in range(PAIRS):
                        last = nc.tensor.matmul(ps[7][:, 0:D], o_T[:, p, :, :].rearrange("p b n -> p (b n)"), wu_sb[:, p, :],
                                                start=(p == 0), stop=(p == PAIRS - 1))
                    last.then_inc(y_done, 1)

            steps(pe, step)

            pe.wait_ge(ffw_ready, 4)
            pe.wait_ge(y_read, TILES)
            with pe.Fori(0, GROUPS) as g:
                pe.wait_ge(f_xn, GT * g + GT)
                for j in range(GT):
                    last = nc.tensor.transpose(ps[6][:, j * P:(j + 1) * P], gxn[:, j, :], ident[:, :])
                last.then_inc(f_t, 1)
                pe.wait_ge(f_lo, g + 1)
                for j in range(GT):
                    for n, (a, w) in enumerate(((gT_lo, wg_lo), (gT_lo, wg_hi), (gT_hi, wg_lo), (gT_hi, wg_hi))):
                        last = nc.tensor.matmul(ps[7][:, j * E:(j + 1) * E], a[:, j * P:(j + 1) * P], w[:, :], start=(n == 0), stop=(n == 3))
                last.then_inc(f_lg, 1)

                def hidden(e):
                    w = (e + E) % NX
                    for c in range(CH):
                        if e > 0:
                            pe.wait_ge(act_ready, NX * CH * g + ((e - 1) * CH + c + 1))
                        fs = slice(c * P, (c + 1) * P)
                        nc.tensor.matmul(ps[c][:, :], w1_hi[:, w, fs], gT_hi[:, :], start=True, stop=False)
                        nc.tensor.matmul(ps[c][:, :], w1_hi[:, w, fs], gT_lo[:, :], start=False, stop=False)
                        nc.tensor.matmul(ps[c][:, :], w1_lo[:, w, fs], gT_hi[:, :], start=False, stop=True).then_inc(h_done, 1)

                hidden(0)
                pe.wait_ge(f_cw, g + 2)
                for j in range(GT):
                    last = nc.tensor.transpose(ps[6][0:NX, j * P:(j + 1) * P], cw[:, j, :], ident[:, :])
                last.then_inc(f_ct, 1)
                pe.wait_ge(f_cT, g + 1)
                for j in range(GT):
                    last = nc.tensor.matmul(ps[7][:, j * D:(j + 1) * D], cwT[:, j * P:(j + 1) * P], b2_sb[:, :], start=True, stop=True)
                last.then_inc(f_bias, 1)
                for e in range(NX):
                    w = (e + E) % NX
                    if e + 1 < NX:
                        hidden(e + 1)
                    pe.wait_ge(act_ready, NX * CH * g + (e + 1) * CH)
                    if e >= 2:
                        pe.wait_ge(fy_read, GT * NX * g + GT * (e - 1))
                    for j in range(GT):
                        for c in range(CH):
                            last = nc.tensor.matmul(ps[4 + e % 2][:, j * D:(j + 1) * D], act[:, e % 2, c, j * P:(j + 1) * P],
                                                    w2_sb[:, w, c, :], start=(c == 0), stop=(c == CH - 1))
                    last.then_inc(fy_done, 1)
                pe.wait_ge(fy_read, GT * NX * g + GT * NX)


_INS = ['x', 'ctx_1024', 'g_xattn', 'g_ffn', 'L0_xattn_Wq', 'L0_xattn_Wk', 'L0_xattn_Wv', 'L0_xattn_Wu', 'L0_xattn_bu',
        'L0_xattn_qn_w', 'L0_xattn_qn_b', 'L0_xattn_kn_w', 'L0_xattn_kn_b', 'L0_ffn_Wg', 'L0_ffn_W1', 'L0_ffn_b1',
        'L0_ffn_W2', 'L0_ffn_b2', 'L0_ffn_Ws1', 'L0_ffn_bs1', 'L0_ffn_Ws2', 'L0_ffn_bs2']
_TRANSPOSED = ('L0_xattn_Wq', 'L0_xattn_Wk', 'L0_xattn_Wv', 'L0_xattn_Wu')
_BY_HIDDEN_UNIT = ('L0_ffn_b1', 'L0_ffn_bs1')


def kernel(**inputs):
    import numpy as np
    import concourse.bacc as bacc
    from concourse.bass_utils import run_bass_kernel_spmd

    nc = bacc.Bacc("TRN2", target_bir_lowering=False, num_devices=1)
    arrays, args = {}, []
    for name in _INS:
        a = np.asarray(inputs[name])
        if name in _TRANSPOSED:
            a = a.T
        if name in _BY_HIDDEN_UNIT:
            a = a.reshape(-1, P).T
        a = np.ascontiguousarray(a)
        arrays[f"in_{name}"] = a
        args.append(nc.dram_tensor(f"in_{name}", a.shape, mybir.dt.from_np(a.dtype), kind="ExternalInput").ap())
    args.append(nc.dram_tensor("out_x", [B, S, D], F32, kind="ExternalOutput").ap())
    flamingo_block(nc, *args)
    r = run_bass_kernel_spmd(nc, [arrays], core_ids=[0])
    return r.results[0]["out_x"]
```

```python
import concourse.bass as bass
from concourse import mybir
from contextlib import ExitStack

F32 = mybir.dt.float32
F32R = mybir.dt.float32r
BF16 = mybir.dt.bfloat16
I32 = mybir.dt.int32
U32 = mybir.dt.uint32
ALU = mybir.AluOpType
ACT = mybir.ActivationFunctionType
AX = mybir.AxisListType

P = 128
B, S, D = 64, 64, 128
HEADS, HD = 16, 64
INNER = HEADS * HD
TOKENS = B * S
TILES = TOKENS // P
PAIRS = HEADS // 2
E, FF = 8, 512
NX = E + 1
CH = FF // P
GT = 4
GROUPS = TILES // GT
GN = GT * P
ROW = D + 1
REGION = TOKENS + P
SPARE = 8
NT = 72
LN_EPS = 1e-5
TOPK_EPS = 1e-9
SHARED = 0.1


def flamingo_block(nc, x, ctx, g_xattn, g_ffn, wqT, wkT, wvT, wuT, bu, qn_w, qn_b, kn_w, kn_b,
                   wg, w1, b1, w2, b2, ws1, bs1, ws2, bs2, out):
    x_v = x.rearrange("b s d -> (b s) d").rearrange("(t p) d -> p t d", p=P)
    ctx_v = ctx.rearrange("b s d -> (b s) d").rearrange("(t p) d -> p t d", p=P)
    out_v = out.rearrange("b s d -> (b s) d").rearrange("(t p) d -> p t d", p=P)

    with ExitStack() as stack:
        def sb(name, shape, dt=F32):
            return stack.enter_context(nc.sbuf_tensor(name, shape, dt))

        def bank(name):
            return stack.enter_context(nc.psum_tensor(name, [P, 512], F32))

        def sem(name):
            return stack.enter_context(nc.semaphore(name))

        x_res = sb("x_res", [P, TILES, D])
        c_in = sb("c_in", [P, 2, D])
        xn = sb("xn", [P, D])
        xc_hi = sb("xc_hi", [P, 2, 2, P], F32R)
        xc_lo = sb("xc_lo", [P, 2, 2, P], F32R)
        w_raw = sb("w_raw", [P, 3, INNER])
        w_hi = sb("w_hi", [P, 3, INNER], F32R)
        w_lo = sb("w_lo", [P, 3, INNER], F32R)
        w_mean = sb("w_mean", [P, 2, HEADS])
        wu_sb = sb("wu_sb", [P, PAIRS, D])
        wide = sb("wide", [P, 4, INNER])
        sq = wide[:, 0:2, :]
        ss = sb("ss", [P, 2, HEADS])
        rstd = sb("rstd", [P, 2, HEADS])
        var_eps = sb("var_eps", [P, 2, HEADS])
        qk_n = wide[:, 2:4, :]
        qk_T = sb("qk_T", [P, 2, PAIRS, P])
        v_sb = sb("v_sb", [P, 2, INNER])
        prob = sb("prob", [P, PAIRS, 2, S])
        spo = sb("spo", [P, 2 * E * (D + 1)])
        prob_T = spo[:, 0:INNER].rearrange("p (a n) -> p a n", a=PAIRS)
        o_T = spo[:, INNER:2 * INNER].rearrange("p (a b n) -> p a b n", a=PAIRS, b=2)
        mx = sb("mx", [P, 2, PAIRS])
        sm = sb("sm", [P, PAIRS * 2])
        rinv = sb("rinv", [P, PAIRS * 2])
        y_tmp = sb("y_tmp", [P, D])
        lnw = sb("lnw", [P, 4])
        gates = sb("gates", [P, 2])
        tg = sb("tg", [P, 2])
        bu_b = sb("bu_b", [P, D])
        tgbu = sb("tgbu", [P, D])
        ident = sb("ident", [P, P])
        expo = sb("expo", [P, 2, HEADS])
        eps = sb("eps", [P, 2, HEADS])
        bn6 = sb("bn6", [P, 6])
        mv = sb("mv", [P, 2])
        xv_eps = sb("xv_eps", [P, 1])
        x_rstd = sb("x_rstd", [P, 1])
        wg_raw = sb("wg_raw", [P, E])
        wg_hi = sb("wg_hi", [P, E], F32R)
        wg_lo = sb("wg_lo", [P, E], F32R)
        w1_raw = sb("w1_raw", [P, NX, FF])
        w1_hi = sb("w1_hi", [P, NX, FF], F32R)
        w1_lo = sb("w1_lo", [P, NX, FF], F32R)
        w2_sb = sb("w2_sb", [P, NX, CH, D])
        bs1_sb = sb("bs1_sb", [P, CH])
        late = w_raw[:, :, :].rearrange("p a n -> p (a n)")
        BC = E * (FF + D) // P
        b_raw = sb("b_raw", [P, BC])
        b_cols = sb("b_cols", [P, 3, BC], BF16)
        b1_parts = sb("b1_parts", [P, E, FF], BF16)
        b2_parts = sb("b2_parts", [P, E, D], BF16)
        rows = late[:, 0:2 * 2 * GT * ROW].rearrange("p (u c j n) -> p u c j n", u=2, c=2, j=GT)
        o = 2 * 2 * GT * ROW
        router = {}
        for name, width in (("lg", GT * E), ("gm", GT), ("gs", GT), ("gtop", GT * 8), ("gidf", GT * 2), ("gw", GT * 2),
                            ("oh", 2 * GT * E), ("rank", GT * E), ("hit", 2 * GT * E), ("slotf", 2 * GT)):
            router[name] = late[:, o:o + width]
            o += width
        assert o <= 3 * INNER
        gp = router["lg"].rearrange("p (j e) -> p j e", j=GT)
        gm, gs = router["gm"], router["gs"]
        gtop = router["gtop"].rearrange("p (j e) -> p j e", j=GT)
        gidf = router["gidf"].rearrange("p (j e) -> p j e", j=GT)
        gw = router["gw"].rearrange("p (j e) -> p j e", j=GT)
        oh = router["oh"].rearrange("p (c j e) -> p c j e", c=2, j=GT)
        rank = router["rank"].rearrange("p (j e) -> p j e", j=GT)
        hit = router["hit"].rearrange("p (c j e) -> p c j e", c=2, j=GT)
        slotf = router["slotf"].rearrange("p (c j) -> p c j", c=2)
        y8 = prob[:, 0:4, :, :].rearrange("p a b n -> p (a b n)")
        gT = sb("gT", [P, 2, GN], F32R)
        gT_hi, gT_lo = gT[:, 0, :], gT[:, 1, :]
        act = wide[:, 0:2, :].rearrange("p a n -> p (a n)").rearrange("p (c n) -> p c n", c=CH)
        gb6 = sb("gb6", [P, GT, 6])
        gmv = sb("gmv", [P, GT, 2])
        gve = sb("gve", [P, GT])
        grs = sb("grs", [P, GT])
        gidx = sb("gidx", [P, GT, 8], U32)
        chosen = sb("chosen", [P, 2, GT, E], BF16)
        total = sb("total", [P, E], BF16)
        run = sb("run", [P, 2, E])
        slot = sb("slot", [P, 2, 2, GT], I32)
        wtok = sb("wtok", [P, TILES, 2])
        iot = sb("iot", [P, E])
        iot_i = sb("iot_i", [P, E], I32)
        ebase = sb("ebase", [P, E])
        ebase_i = sb("ebase_i", [P, E], I32)
        tok_i = sb("tok_i", [P, 2, TILES], I32)
        before = sb("before", [P, P], BF16)
        ones_b = sb("ones_b", [P, P], BF16)
        rows3 = sb("rows3", [P, P], BF16)
        tgbs2 = sb("tgbs2", [P, D])
        tg01 = sb("tg01", [P, 1])
        nt = sb("nt", [P, E])
        big = sb("big", [P, E, 32])
        cum = sb("cum", [P, 2, E])
        tile_n = sb("tile_n", [P, NT])
        past = sb("past", [P, NT, E])
        sched = sb("sched", [P, 3, NT])
        sched_i = sb("sched_i", [P, 2, NT], I32)
        cnt_i = sb("cnt_i", [P, E], I32)
        i32s = sb("i32s", [P, 256], I32)
        pad = spo[:, :].rearrange("p (k n) -> p k n", n=ROW)
        xs_in = v_sb[:, :, :].rearrange("p a n -> p (a n)")[:, 0:4 * ROW].rearrange("p (k n) -> p k n", k=4)
        xs_hi = sb("xs_hi", [P, 2, P], F32R)
        xs_lo = sb("xs_lo", [P, 2, P], F32R)
        xs_ix = sb("xs_ix", [P, 4], I32)
        hid = qk_T[:, :, :, :].rearrange("p a b n -> p (a b n)")[:, 0:2 * FF].rearrange("p (a n) -> p a n", a=2)
        hid_T = qk_T[:, :, :, :].rearrange("p a b n -> p (a b n)")[:, 2 * FF:4 * FF].rearrange("p (a n) -> p a n", a=2)
        yb = o_T[:, :, :, :].rearrange("p a b n -> p (a b n)")[:, 0:4 * D].rearrange("p (k n) -> p k n", k=4)
        y_in = wide[:, :, :].rearrange("p a n -> p (a n)")[:, 0:4 * GN].rearrange("p (u c j n) -> p u c j n", u=2, c=2, j=GT)

        ps = [bank(f"ps{i}") for i in range(8)]

        const_in, wq_in, wu_in, ffw_in = sem("const_in"), sem("wq_in"), sem("wu_in"), sem("ffw_in")
        x_in = sem("x_in")
        c_loaded = [sem("c_loaded0"), sem("c_loaded1")]
        ones_ready, ident_ready, expo_ready = sem("ones_ready"), sem("ident_ready"), sem("expo_ready")
        wprep, w_ready, tanh_ready, tgbu_ready = sem("wprep"), sem("w_ready"), sem("tanh_ready"), sem("tgbu_ready")
        bn_done, mv_ready, xve_ready, xrs_ready, xn_ready = (sem(n) for n in ("bn_done", "mv_ready", "xve_ready", "xrs_ready", "xn_ready"))
        xt_done, xhi_ready, xlo_ready = sem("xt_done"), sem("xhi_ready"), sem("xlo_ready")
        proj_done, sq_ready, ss_ready, ve_ready, rstd_ready, qn_ready = (
            sem(n) for n in ("proj_done", "sq_ready", "ss_ready", "ve_ready", "rstd_ready", "qn_ready"))
        qt_done, kt_done, qT_ready, kT_ready = sem("qt_done"), sem("kt_done"), sem("qT_ready"), sem("kT_ready")
        v_done, v_ready = sem("v_done"), sem("v_ready")
        s_done, mx_ready, sub_ready, exp_ready, sum_ready, rinv_ready, p_ready = (
            sem(n) for n in ("s_done", "mx_ready", "sub_ready", "exp_ready", "sum_ready", "rinv_ready", "p_ready"))
        pt_done, pt0_ready, pt1_ready = sem("pt_done"), sem("pt0_ready"), sem("pt1_ready")
        o_done, o_ready, y_done, y_read, x1_ready = (sem(n) for n in ("o_done", "o_ready", "y_done", "y_read", "x1_ready"))
        f_bn, f_mv, f_ve, f_rs, f_xn, f_row = (sem(n) for n in ("f_bn", "f_mv", "f_ve", "f_rs", "f_xn", "f_row"))
        f_t, f_hi, f_lo, f_lg, f_dve, f_exp, f_ab = (sem(n) for n in ("f_t", "f_hi", "f_lo", "f_lg", "f_dve", "f_exp", "f_ab"))
        f_ab2, f_c, rows3_ready = sem("f_ab2"), sem("f_c"), sem("rows3_ready")
        f_rank, f_slot, f_sent, h_done, act_ready, fy_done, f_x2 = (
            sem(n) for n in ("f_rank", "f_slot", "f_sent", "h_done", "act_ready", "fy_done", "f_x2"))
        ffw_ready, bias_in, bias_prep, bias_ready, gp_const, pad_ready, run0 = (
            sem(n) for n in ("ffw_ready", "bias_in", "bias_prep", "bias_ready", "gp_const", "pad_ready", "run0"))
        sc_step, sched_ready, padded = sem("sc_step"), sem("sched_ready"), sem("padded")
        r_in = [sem(f"r_in{k}") for k in range(4)]
        r_t, r_hi, r_lo, r_ix, r_h, r_act, r_ta, r_aT, r_y, r_yb = (
            sem(n) for n in ("r_t", "r_hi", "r_lo", "r_ix", "r_h", "r_act", "r_ta", "r_aT", "r_y", "r_yb"))
        r_sent = [sem(f"r_sent{k}") for k in range(4)]
        o_in, o_a, o_b = [[sem("o_in0"), sem("o_in1")], sem("o_a"), sem("o_b")]
        o_stored = sem("o_stored")

        routed = nc.dram_tensor("routed", [E * REGION + SPARE * P, ROW], F32, kind="Internal").ap()
        bias1 = nc.dram_tensor("bias1", [3, E * FF], BF16, kind="Internal").ap()
        bias2 = nc.dram_tensor("bias2", [3, E * D], BF16, kind="Internal").ap()
        results = nc.dram_tensor("results", [2 * TOKENS + 2 * E * P, D], F32, kind="Internal").ap()

        block = stack.enter_context(nc.Block())

        STEADY = range(2, TILES - 2)

        def steps(eng, step):
            for s in range(-2, STEADY.start):
                step(s, s % 2, s)
            with eng.Fori(0, len(STEADY) // 2) as i:
                for half in range(2):
                    step(2 * i + (STEADY.start + half), half, STEADY.start)
            for s in range(STEADY.stop, TILES + 1):
                step(s, s % 2, s)

        def wait_apart(eng, semaphore, value, *more):
            waits = [(semaphore, value), *more]
            for _, count in waits:
                if not isinstance(count, int):
                    eng.compute_val(count)
            eng.wait_ge(ident_ready, 1)
            for which, count in waits:
                eng.wait_ge(which, count)

        def has(s):
            return 0 <= s < TILES

        def groups(eng, group):
            group(0, 0, False)
            with eng.Fori(0, GROUPS // 2 - 1) as i:
                for half in range(2):
                    group(2 * i + (1 + half), 1 - half, False)
            group(GROUPS - 1, (GROUPS - 1) % 2, True)

        ROUTED = range(2, NT - 2)

        def row_steps(eng, step):
            for n in range(-2, ROUTED.start):
                step(n, n % 4, n)
            with eng.Fori(0, len(ROUTED) // 4) as i:
                for u in range(4):
                    step(4 * i + (ROUTED.start + u), (ROUTED.start + u) % 4, ROUTED.start)
            for n in range(ROUTED.stop, NT + 1):
                step(n, n % 4, n)

        def tile_of_sched(what, n):
            return sched_i[0:1, what, n:n + 1] if isinstance(n, int) else sched_i[0:1, what, bass.ds(n, 1)]

        def is_row_tile(n):
            return 0 <= n < NT

        def tile_of(a, t):
            return a[:, t, :] if isinstance(t, int) else a[:, bass.ds(t, 1), :].rearrange("p a d -> p (a d)")

        @block.sync
        def _(sp):
            for c in range(4):
                n = TILES // 4
                sp.dma_start(x_res[:, c * n:(c + 1) * n, :], x_v[:, c * n:(c + 1) * n, :]).then_inc(x_in, 16)
                if c == 0:
                    for t in range(2):
                        sp.dma_start(c_in[:, t, :], ctx_v[:, t, :]).then_inc(c_loaded[t], 16)
                    for n_, w in enumerate((wqT, wkT, wvT)):
                        sp.dma_start(w_raw[:, n_, :], w).then_inc(wq_in, 16)
            sp.dma_start(wu_sb[:, :, :], wuT.rearrange("(c p) n -> p c n", p=P)).then_inc(wu_in, 16)
            sp.dma_start(wg_raw[:, :], wg).then_inc(ffw_in, 16)
            sp.dma_start(w1_raw[:, 0:E, :], w1.rearrange("e h f -> h e f")).then_inc(ffw_in, 16)
            sp.dma_start(w1_raw[:, E, :], ws1).then_inc(ffw_in, 16)
            sp.dma_start(w2_sb[:, 0:E, :, :].rearrange("p e c n -> p (e c) n"),
                         w2.rearrange("e f h -> (e f) h").rearrange("(k p) n -> p k n", p=P)).then_inc(ffw_in, 16)
            sp.dma_start(w2_sb[:, E, :, :], ws2.rearrange("(c p) n -> p c n", p=P)).then_inc(ffw_in, 16)
            sp.dma_start(bs1_sb[:, :], bs1).then_inc(ffw_in, 16)
            with sp.Fori(0, TILES // 2 - 1) as i:
                for half in range(2):
                    sp.compute_val(2 * i + (half + 2))
                    wait_apart(sp, xt_done, 2 * i + (half + 1))
                    sp.dma_start(c_in[:, half, :], ctx_v[:, bass.ds(2 * i + (half + 2), 1), :].rearrange("p a d -> p (a d)")
                                 ).then_inc(c_loaded[half], 16)
            sp.wait_ge(sched_ready, 1)
            sp.wait_ge(pad_ready, 2)
            for e in range(E):
                count = sp.value_load(cnt_i[0:1, e:e + 1], min_val=0, max_val=TOKENS)
                sp.dma_start(routed[bass.ds(count + e * REGION, P), :], pad[:, e, :]).then_inc(padded, 16)
            sp.dma_start(routed[E * REGION:E * REGION + SPARE * P, :].rearrange("(k p) n -> p k n", p=P), pad[:, E:2 * E, :]).then_inc(padded, 16)
            sp.wait_ge(padded, 16 * (E + 1))
            sp.wait_ge(f_sent, 16 * 2 * GT * GROUPS)

            def step(n, q, k):
                if is_row_tile(k + 2):
                    row = sp.value_load(tile_of_sched(1, n + 2), min_val=0, max_val=E * REGION + SPARE * P - P)
                    if k + 2 >= 4:
                        sp.wait_ge(r_t, n - 1)
                        sp.wait_ge(r_ix, n - 1)
                    b4 = (q + 2) % 4
                    sp.dma_start(xs_in[:, b4, :], routed[bass.ds(row, P), :]).then_inc(r_in[b4], 16)

            row_steps(sp, step)

            for k in range(4):
                sp.wait_ge(r_sent[k], 16 * (NT // 4))
            res_v = results[0:2 * TOKENS, :].rearrange("(c t p) d -> p c t d", c=2, p=P)
            for g in range(GROUPS):
                if g >= 2:
                    sp.wait_ge(o_b, GT * (g - 1))
                for c in range(2):
                    sp.dma_start(y_in[:, g % 2, c, :, :], res_v[:, c, GT * g:GT * g + GT, :]).then_inc(o_in[g % 2], 16)
            sp.wait_ge(o_stored, 16 * GROUPS)

        @block.scalar
        def _(sc):
            for n, src in enumerate((g_xattn, g_ffn)):
                sc.dma_start(gates[:, n:n + 1], src.rearrange("(a n) -> a n", a=1).partition_broadcast(P).rearrange("p a n -> p (a n)")).then_inc(const_in, 16)
            sc.dma_start(bu_b[:, :], bu.rearrange("(a n) -> a n", a=1).partition_broadcast(P).rearrange("p a n -> p (a n)")).then_inc(const_in, 16)
            for n, src in enumerate((qn_w, qn_b, kn_w, kn_b)):
                for h in range(2):
                    sc.dma_start(lnw[h * HD:(h + 1) * HD, n:n + 1], src.rearrange("(p a) -> p a", a=1)).then_inc(const_in, 16)
            sc.dma_start(tgbs2[:, :], bs2.rearrange("(a n) -> a n", a=1).partition_broadcast(P).rearrange("p a n -> p (a n)")).then_inc(const_in, 16)
            sc.wait_ge(const_in, 12 * 16)
            nc.scalar.activation(tg[:, :], gates[:, :], ACT.Tanh).then_inc(tanh_ready, 1)

            def step(s, par, k):
                if has(k):
                    for j in range(2):
                        sc.wait_ge(qt_done, 2 * s + (j + 1))
                        nc.scalar.activation(qk_T[:, 0, 4 * j:4 * j + 4, :].rearrange("p a n -> p (a n)"), ps[6 + j][:, :],
                                             ACT.Identity, bias=lnw[:, 1:2], scale=lnw[:, 0:1]).then_inc(qT_ready, 1)
                if has(k + 1):
                    if k + 1 >= 1:
                        sc.wait_ge(ss_ready, 2 * s + 2)
                    for j in range(4):
                        sc.wait_ge(proj_done, 4 * s + (5 + j))
                        nc.scalar.activation(sq[:, j // 2, (j % 2) * 512:(j % 2) * 512 + 512], ps[j][:, :],
                                             ACT.Square, scale=HD ** -0.5).then_inc(sq_ready, 1)
                if has(k):
                    if k >= 2:
                        sc.wait_ge(o_done, 2 * s - 2)
                    for j in range(2):
                        sc.wait_ge(v_done, 2 * s + (j + 1))
                        nc.scalar.activation(v_sb[:, par, j * 512:(j + 1) * 512], ps[4 + j][:, :], ACT.Copy).then_inc(v_ready, 1)
                if has(k - 1):
                    sc.wait_ge(pt_done, 2 * s - 1)
                    nc.scalar.activation(prob_T[:, 0:4, :].rearrange("p a n -> p (a n)"), ps[6][:, :], ACT.Copy).then_inc(pt0_ready, 1)
                if has(k):
                    sc.wait_ge(sub_ready, 2 * s + 2)
                    p_all = prob[:, :, :, :].rearrange("p a b n -> p (a b n)")
                    nc.scalar.activation(p_all, p_all, ACT.Exp, scale=HD ** -0.5).then_inc(exp_ready, 1)
                if has(k - 1):
                    if k >= 2:
                        sc.wait_ge(y_done, s - 1)
                    for j in range(2):
                        sc.wait_ge(o_done, 2 * s + (j - 1))
                        nc.scalar.activation(o_T[:, :, j, :], ps[6 + j][:, :].rearrange("p (a n) -> p a n", a=PAIRS),
                                             ACT.Copy).then_inc(o_ready, 1)
                if has(k + 2):
                    sc.wait_ge(xt_done, s + 3)
                    nc.scalar.activation(xc_hi[:, par, :, :].rearrange("p a n -> p (a n)"), ps[6][:, 0:256], ACT.Copy).then_inc(xhi_ready, 1)

            steps(sc, step)

            def group(g, par, last):
                sc.wait_ge(f_t, g + 1)
                nc.scalar.activation(gT_hi, ps[6][:, :], ACT.Copy).then_inc(f_hi, 1)
                sc.wait_ge(f_dve, 15 * g + 2)
                nc.scalar.activation(gp, gp, ACT.Exp).then_inc(f_exp, 1)
                for c in range(CH):
                    sc.wait_ge(h_done, CH * g + (c + 1))
                    nc.scalar.activation(act[:, c, :], ps[c][:, :], ACT.Silu, bias=bs1_sb[:, c:c + 1]).then_inc(act_ready, 1)

            groups(sc, group)

            def row_step(n, q, k):
                par = q % 2
                if is_row_tile(k + 1):
                    if k + 1 >= 2:
                        sc.wait_ge(r_ta, n)
                    sc.wait_ge(r_h, n + 2)
                    nc.scalar.activation(hid[:, 1 - par, :], ps[1 - par][:, :], ACT.Silu).then_inc(r_act, 1)
                if is_row_tile(k + 2):
                    sc.wait_ge(r_t, n + 3)
                    nc.scalar.activation(xs_hi[:, par, :], ps[6 + par][:, 0:P], ACT.Copy).then_inc(r_hi, 1)
                if is_row_tile(k - 1):
                    b4 = (q - 1) % 4
                    sc.wait_ge(r_y, n)
                    if k - 1 >= 4:
                        sc.wait_ge(r_sent[b4], 4 * (n - 1 - b4) if isinstance(n, int) else 4 * (n - (1 + b4)))
                    nc.scalar.activation(yb[:, b4, :], ps[4 + (1 - par)][:, 0:D], ACT.Copy).then_inc(r_yb, 1)

            row_steps(sc, row_step)
            for g in range(GROUPS):
                sc.wait_ge(o_b, GT * (g + 1))
                sc.dma_start(out_v[:, GT * g:GT * (g + 1), :], x_res[:, GT * g:GT * (g + 1), :]).then_inc(o_stored, 16)

        @block.gpsimd
        def _(gp_):
            nc.gpsimd.memset(ident[:, :], 0.0).then_inc(ones_ready, 1)
            gp_.wait_ge(ones_ready, 1)
            nc.gpsimd.affine_select(out=ident[:, :], in_=ident[:, :], compare_op=ALU.not_equal, fill=1.0,
                                    base=0, pattern=[[-1, P]], channel_multiplier=1).then_inc(ident_ready, 1)
            nc.gpsimd.memset(expo[:, :, :], -0.5).then_inc(expo_ready, 1)
            nc.gpsimd.memset(eps[:, :, :], LN_EPS).then_inc(expo_ready, 1)
            nc.gpsimd.iota(iot_i[:, :], pattern=[[1, E]], base=0, channel_multiplier=0).then_inc(expo_ready, 1)
            nc.gpsimd.iota(ebase_i[:, :], pattern=[[REGION, E]], base=0, channel_multiplier=0).then_inc(expo_ready, 1)
            nc.gpsimd.iota(tok_i[:, :, :], pattern=[[TOKENS, 2], [P, TILES]], base=0, channel_multiplier=1).then_inc(expo_ready, 1)
            nc.gpsimd.iota(i32s[:, 0:NT], pattern=[[1, NT]], base=0, channel_multiplier=0).then_inc(expo_ready, 1)
            nc.gpsimd.iota(i32s[:, 128:160], pattern=[[P, 32]], base=0, channel_multiplier=0).then_inc(expo_ready, 1)
            nc.gpsimd.iota(i32s[:, 200:200 + 2 * E], pattern=[[P, 2 * E]], base=2 * TOKENS, channel_multiplier=1).then_inc(expo_ready, 1)
            nc.gpsimd.memset(ones_b[:, :], 1.0).then_inc(expo_ready, 1)
            nc.gpsimd.memset(before[:, :], 1.0).then_inc(expo_ready, 1)
            gp_.wait_ge(expo_ready, 10)
            nc.gpsimd.tensor_copy(iot[:, :], iot_i[:, :]).then_inc(gp_const, 1)
            nc.gpsimd.tensor_copy(ebase[:, :], ebase_i[:, :]).then_inc(gp_const, 1)
            nc.gpsimd.tensor_copy(tile_n[:, :], i32s[:, 0:NT]).then_inc(gp_const, 1)
            nc.gpsimd.tensor_copy(big[:, 0, :], i32s[:, 128:160]).then_inc(gp_const, 1)
            nc.gpsimd.affine_select(out=before[:, :], in_=before[:, :], compare_op=ALU.is_gt, fill=0.0,
                                    base=0, pattern=[[1, P]], channel_multiplier=-1).then_inc(gp_const, 1)
            n1 = E * FF // P
            gp_.dma_start(b_raw[:, 0:n1], b1.rearrange("e f -> (e f)").rearrange("(p n) -> p n", p=P)).then_inc(bias_in, 16)
            gp_.dma_start(b_raw[:, n1:BC], b2.rearrange("e f -> (e f)").rearrange("(p n) -> p n", p=P)).then_inc(bias_in, 16)
            nc.gpsimd.memset(b1_parts[:, :, :], 0.0).then_inc(bias_prep, 1)
            nc.gpsimd.memset(b2_parts[:, :, :], 0.0).then_inc(bias_prep, 1)
            gp_.wait_ge(bias_in, 32)
            done = 2
            for n in range(3):
                if n > 0:
                    gp_.wait_ge(bias_prep, done)
                    nc.gpsimd.tensor_tensor(b_raw[:, :], b_raw[:, :], b_cols[:, n - 1, :], ALU.subtract).then_inc(bias_prep, 1)
                    done += 1
                    gp_.wait_ge(bias_prep, done)
                nc.gpsimd.tensor_copy(b_cols[:, n, :], b_raw[:, :]).then_inc(bias_prep, 1)
                done += 1
            gp_.wait_ge(bias_prep, done)
            for lo, hi, dram in ((0, n1, bias1), (n1, BC, bias2)):
                gp_.dma_start(dram.rearrange("a (p n) -> p a n", p=P), b_cols[:, :, lo:hi]).then_inc(bias_in, 16)
            gp_.wait_ge(bias_in, 64)
            for n in range(3):
                at = slice(32 * n, 32 * n + 1)
                gp_.dma_start(b1_parts[at, :, :].rearrange("p e n -> p (e n)"), bias1[n:n + 1, :]).then_inc(bias_ready, 16)
                gp_.dma_start(b2_parts[at, :, :].rearrange("p e n -> p (e n)"), bias2[n:n + 1, :]).then_inc(bias_ready, 16)

            def step(s, par, k):
                if has(k + 2):
                    gp_.wait_ge(mv_ready, s + 3)
                    nc.gpsimd.tensor_tensor(xv_eps[:, :], mv[:, 1:2], eps[:, 0, 0:1], ALU.add).then_inc(xve_ready, 1)
                    gp_.wait_ge(xve_ready, s + 3)
                    nc.gpsimd.tensor_tensor(x_rstd[:, :], xv_eps[:, :], expo[:, 0, 0:1], ALU.pow).then_inc(xrs_ready, 1)
                if has(k + 1):
                    for n in range(2):
                        gp_.wait_ge(ss_ready, 2 * s + (3 + n))
                        nc.gpsimd.tensor_tensor(var_eps[:, n, :], ss[:, n, :], eps[:, n, :], ALU.add).then_inc(ve_ready, 1)
                        gp_.wait_ge(ve_ready, 2 * s + (3 + n))
                        nc.gpsimd.tensor_tensor(rstd[:, n, :], var_eps[:, n, :], expo[:, n, :], ALU.pow).then_inc(rstd_ready, 1)
                if has(k):
                    gp_.wait_ge(rinv_ready, s + 1)
                    pv = prob[:, :, :, :].rearrange("p a b n -> p (a b) n")
                    nc.gpsimd.tensor_tensor(pv, pv, rinv[:, :].unsqueeze(2).to_broadcast([P, 2 * PAIRS, S]), ALU.mult).then_inc(p_ready, 1)

            steps(gp_, step)

            gp_.wait_ge(ffw_in, 6 * 16)
            nc.gpsimd.tensor_copy(w1_hi[:, :, :], w1_raw[:, :, :]).then_inc(ffw_ready, 1)
            nc.gpsimd.tensor_copy(wg_hi[:, :], wg_raw[:, :]).then_inc(ffw_ready, 1)
            gp_.wait_ge(ffw_ready, 2)
            nc.gpsimd.tensor_tensor(w1_lo[:, :, :], w1_raw[:, :, :], w1_hi[:, :, :].bitcast(F32), ALU.subtract).then_inc(ffw_ready, 1)
            nc.gpsimd.tensor_tensor(wg_lo[:, :], wg_raw[:, :], wg_hi[:, :].bitcast(F32), ALU.subtract).then_inc(ffw_ready, 1)
            def norm2(g):
                gp_.wait_ge(f_mv, GT * g + GT)
                nc.gpsimd.tensor_tensor(gve[:, :], gmv[:, :, 1], eps[:, 0, 0:GT], ALU.add).then_inc(f_ve, 1)
                gp_.wait_ge(f_ve, g + 1)
                nc.gpsimd.tensor_tensor(grs[:, :], gve[:, :], expo[:, 0, 0:GT], ALU.pow).then_inc(f_rs, 1)

            def group(g, par, last):
                if not last:
                    norm2(g + 1)
                wait_apart(gp_, f_slot, g + 1, (f_row, 2 * g + 2))
                for c in range(2):
                    for j in range(GT):
                        gp_.indirect_dma_start(out=routed[:, :], out_offset=bass.IndirectOffsetOnAxis(ap=slot[:, par, c, j:j + 1], axis=0),
                                               in_=rows[:, par, c, j, :], in_offset=None).then_inc(f_sent, 16)

            gp_.wait_ge(y_done, TILES)
            nc.gpsimd.memset(pad[:, :, :], 0.0).then_inc(pad_ready, 1)
            gp_.wait_ge(pad_ready, 1)
            nc.gpsimd.tensor_copy(pad[:, :, D].bitcast(I32), i32s[:, 200:200 + 2 * E]).then_inc(pad_ready, 1)
            norm2(0)
            groups(gp_, group)

            def row_step(n, q, k):
                if is_row_tile(k - 1):
                    b4 = (q - 1) % 4
                    wait_apart(gp_, r_yb, n)
                    gp_.indirect_dma_start(out=results[:, :], out_offset=bass.IndirectOffsetOnAxis(ap=xs_ix[:, b4:b4 + 1], axis=0),
                                           in_=yb[:, b4, :], in_offset=None).then_inc(r_sent[b4], 16)

            row_steps(gp_, row_step)

        @block.vector
        def _(ve):
            ve.wait_ge(wq_in, 48)
            for n in range(2):
                nc.vector.tensor_reduce(w_mean[:, n, :], w_raw[:, n, :].rearrange("p (h d) -> p h d", h=HEADS), AX.X, ALU.add).then_inc(wprep, 1)
            ve.wait_ge(wprep, 2)
            nc.vector.tensor_scalar(w_mean[:, :, :], w_mean[:, :, :], 1.0 / HD, None, ALU.mult).then_inc(wprep, 1)
            ve.wait_ge(wprep, 3)
            for n in range(2):
                wv_ = w_raw[:, n, :].rearrange("p (h d) -> p h d", h=HEADS)
                nc.vector.tensor_tensor(wv_, wv_, w_mean[:, n, :].unsqueeze(2).to_broadcast([P, HEADS, HD]), ALU.subtract).then_inc(wprep, 1)
            ve.wait_ge(wprep, 5)
            nc.vector.tensor_copy(w_hi[:, :, :], w_raw[:, :, :]).then_inc(wprep, 1)
            ve.wait_ge(wprep, 6)
            nc.vector.tensor_tensor(w_lo[:, :, :], w_raw[:, :, :], w_hi[:, :, :].bitcast(F32), ALU.subtract).then_inc(w_ready, 1)
            ve.wait_ge(tanh_ready, 1)
            nc.vector.tensor_scalar(tgbu[:, :], bu_b[:, :], tg[:, 0:1], None, ALU.mult).then_inc(tgbu_ready, 1)
            ve.wait_ge(x_in, 64)

            def step(s, par, k):
                if has(k + 2):
                    if k + 2 >= 1:
                        ve.wait_ge(xn_ready, s + 2)
                    xt = x_res[:, s + 2, :] if isinstance(s, int) else x_res[:, bass.ds(s + 2, 1), :].rearrange("p a d -> p (a d)")
                    nc.vector.bn_stats(bn6[:, :], xt).then_inc(bn_done, 1)
                    wait_apart(ve, bn_done, s + 3)
                    nc.vector.bn_aggr(mv[:, :], bn6[:, :]).then_inc(mv_ready, 1)
                if has(k):
                    for j in range(2):
                        ve.wait_ge(kt_done, 2 * s + (j + 1))
                        nc.vector.tensor_scalar(qk_T[:, 1, 4 * j:4 * j + 4, :].rearrange("p a n -> p (a n)"), ps[6 + j][:, :],
                                                lnw[:, 2:3], lnw[:, 3:4], ALU.mult, ALU.add).then_inc(kT_ready, 1)
                if has(k + 2):
                    ve.wait_ge(xrs_ready, s + 3)
                    if k + 2 >= 1:
                        ve.wait_ge(xt_done, s + 2)
                    nc.vector.tensor_scalar(xn[:, :], xt, mv[:, 0:1], x_rstd[:, 0:1], ALU.subtract, ALU.mult).then_inc(xn_ready, 1)
                if has(k + 1):
                    for n in range(2):
                        ve.wait_ge(sq_ready, 4 * s + (6 + 2 * n))
                        if k + 1 >= 1:
                            ve.wait_ge(ve_ready, 2 * s + (1 + n))
                        nc.vector.tensor_reduce(ss[:, n, :], sq[:, n, :].rearrange("p (h d) -> p h d", h=HEADS), AX.X, ALU.add).then_inc(ss_ready, 1)
                if has(k - 1):
                    ve.wait_ge(pt_done, 2 * s)
                    nc.vector.tensor_copy(prob_T[:, 4:8, :].rearrange("p a n -> p (a n)"), ps[7][:, :]).then_inc(pt1_ready, 1)
                if has(k + 1):
                    for j in range(4):
                        n, half = j // 2, j % 2
                        ve.wait_ge(rstd_ready, 2 * s + (3 + n))
                        if k >= 0:
                            ve.wait_ge(kt_done, 2 * s + 2)
                        nc.vector.tensor_tensor(
                            qk_n[:, n, half * 512:(half + 1) * 512].rearrange("p (h d) -> p h d", h=8),
                            ps[j][:, :].rearrange("p (h d) -> p h d", h=8),
                            rstd[:, n, half * 8:half * 8 + 8].unsqueeze(2).to_broadcast([P, 8, HD]), ALU.mult).then_inc(qn_ready, 1)
                if has(k):
                    if k >= 1:
                        ve.wait_ge(pt_done, 2 * s)
                    for j in range(2):
                        ve.wait_ge(s_done, 2 * s + (j + 1))
                        sv = ps[4 + j][:, :].rearrange("p (a n) -> p a n", a=PAIRS)
                        nc.vector.tensor_reduce(mx[:, j, :], sv, AX.X, ALU.max).then_inc(mx_ready, 1)
                        ve.wait_ge(mx_ready, 2 * s + (j + 1))
                        nc.vector.tensor_tensor(prob[:, :, j, :], sv, mx[:, j, :].unsqueeze(2).to_broadcast([P, PAIRS, S]),
                                                ALU.subtract).then_inc(sub_ready, 1)
                    ve.wait_ge(exp_ready, s + 1)
                    nc.vector.tensor_reduce(sm[:, :], prob[:, :, :, :].rearrange("p a b n -> p (a b) n"), AX.X, ALU.add).then_inc(sum_ready, 1)
                    ve.wait_ge(sum_ready, s + 1)
                    if k >= 1:
                        ve.wait_ge(p_ready, s)
                    nc.vector.reciprocal(rinv[:, :], sm[:, :]).then_inc(rinv_ready, 1)
                if has(k + 2):
                    ve.wait_ge(xhi_ready, s + 3)
                    nc.vector.tensor_tensor(xc_lo[:, par, :, :].rearrange("p a n -> p (a n)"), ps[6][:, 0:256],
                                            xc_hi[:, par, :, :].rearrange("p a n -> p (a n)").bitcast(F32), ALU.subtract).then_inc(xlo_ready, 1)
                if has(k - 1):
                    ve.wait_ge(y_done, s)
                    xs = x_res[:, s - 1, :] if isinstance(s, int) else x_res[:, bass.ds(s - 1, 1), :].rearrange("p a d -> p (a d)")
                    if k >= 2:
                        ve.wait_ge(x1_ready, s - 1)
                    nc.vector.scalar_tensor_tensor(y_tmp[:, :], ps[7][:, 0:D], tg[:, 0:1], tgbu[:, :], ALU.mult, ALU.add).then_inc(y_read, 1)
                    ve.wait_ge(y_read, s)
                    nc.vector.tensor_tensor(xs, xs, y_tmp[:, :], ALU.add).then_inc(x1_ready, 1)

            ve.wait_ge(tgbu_ready, 1)
            steps(ve, step)
            ve.wait_ge(x1_ready, TILES)
            nc.vector.tensor_scalar(tg01[:, :], tg[:, 1:2], SHARED, None, ALU.mult).then_inc(run0, 1)
            nc.vector.memset(run[:, 0, :], 0.0).then_inc(run0, 1)
            nc.vector.memset(rows3[:, :], 0.0).then_inc(run0, 1)
            ve.wait_ge(run0, 3)
            for n in range(3):
                nc.vector.memset(rows3[32 * n:32 * n + 1, :], 1.0).then_inc(rows3_ready, 1)
            nc.vector.tensor_scalar(tgbs2[:, :], tgbs2[:, :], tg01[:, 0:1], None, ALU.mult).then_inc(run0, 1)
            ve.wait_ge(run0, 4)
            ve.wait_ge(gp_const, 5)

            def norm2(g, par, reused=False):
                for j in range(GT):
                    nc.vector.bn_stats(gb6[:, j, :], tile_of(x_res, GT * g + j)).then_inc(f_bn, 1)
                for j in range(GT):
                    wait_apart(ve, f_bn, GT * g + (j + 1))
                    nc.vector.bn_aggr(gmv[:, j, :], gb6[:, j, :]).then_inc(f_mv, 1)
                ve.wait_ge(f_rs, g + 1)
                if reused:
                    ve.wait_ge(f_sent, 2 * GT * 16 * (g - 1))
                for j in range(GT):
                    nc.vector.tensor_scalar(rows[:, par, 0, j, 0:D], tile_of(x_res, GT * g + j), gmv[:, j, 0:1], grs[:, j:j + 1],
                                            ALU.subtract, ALU.mult).then_inc(f_xn, 1)

            def group(g, par, last):
                ve.wait_ge(f_xn, GT * g + GT)
                nc.vector.tensor_copy(rows[:, par, 1, :, 0:D], rows[:, par, 0, :, 0:D]).then_inc(f_row, 1)
                dest = tok_i[:, :, GT * g:GT * g + GT] if isinstance(g, int) else tok_i[:, :, bass.ds(GT * g, GT)]
                nc.vector.tensor_copy(rows[:, par, :, :, D].bitcast(I32), dest).then_inc(f_row, 1)
                ve.wait_ge(f_hi, g + 1)
                nc.vector.tensor_tensor(gT_lo, ps[6][:, :], gT_hi.bitcast(F32), ALU.subtract).then_inc(f_lo, 1)
                ve.wait_ge(f_lg, g + 1)
                lg = ps[7][:, 0:GT * E].rearrange("p (j e) -> p j e", j=GT)
                nc.vector.tensor_reduce(gm, lg, AX.X, ALU.max).then_inc(f_dve, 1)
                ve.wait_ge(f_dve, 15 * g + 1)
                nc.vector.tensor_tensor(gp, lg, gm.unsqueeze(2).to_broadcast([P, GT, E]), ALU.subtract).then_inc(f_dve, 1)
                if not last:
                    norm2(g + 1, 1 - par, not (isinstance(g, int) and g == 0))
                ve.wait_ge(f_exp, g + 1)
                nc.vector.tensor_reduce(gs, gp, AX.X, ALU.add).then_inc(f_dve, 1)
                ve.wait_ge(f_dve, 15 * g + 3)
                nc.vector.reciprocal(gs, gs).then_inc(f_dve, 1)
                ve.wait_ge(f_dve, 15 * g + 4)
                nc.vector.tensor_tensor(gp, gp, gs.unsqueeze(2).to_broadcast([P, GT, E]), ALU.mult).then_inc(f_dve, 1)
                wait_apart(ve, f_dve, 15 * g + 5)
                for j in range(GT):
                    nc.vector.max(gtop[:, j, :], gp[:, j, :]).then_inc(f_ab, 1)
                wait_apart(ve, f_ab, 2 * GT * g + GT)
                for j in range(GT):
                    nc.vector.max_index(gidx[:, j, :], gtop[:, j, :], gp[:, j, :]).then_inc(f_ab, 1)
                nc.vector.tensor_reduce(gs, gtop[:, :, 0:2], AX.X, ALU.add).then_inc(f_dve, 1)
                ve.wait_ge(f_dve, 15 * g + 6)
                nc.vector.tensor_scalar(gs, gs, TOPK_EPS, None, ALU.add).then_inc(f_dve, 1)
                ve.wait_ge(f_dve, 15 * g + 7)
                nc.vector.reciprocal(gs, gs).then_inc(f_dve, 1)
                ve.wait_ge(f_dve, 15 * g + 8)
                nc.vector.tensor_tensor(gw, gtop[:, :, 0:2], gs.unsqueeze(2).to_broadcast([P, GT, 2]), ALU.mult).then_inc(f_dve, 1)
                ve.wait_ge(f_ab, 2 * GT * g + 2 * GT)
                nc.vector.tensor_copy(gidf, gidx[:, :, 0:2]).then_inc(f_dve, 1)
                ve.wait_ge(f_dve, 15 * g + 10)
                wt = wtok[:, GT * g:GT * g + GT, :] if isinstance(g, int) else wtok[:, bass.ds(GT * g, GT), :]
                nc.vector.tensor_scalar(wt, gw, tg[:, 1:2], None, ALU.mult).then_inc(f_ab2, 1)
                for c in range(2):
                    nc.vector.tensor_tensor(oh[:, c, :, :], iot[:, :].unsqueeze(1).to_broadcast([P, GT, E]),
                                            gidf[:, :, c].unsqueeze(2).to_broadcast([P, GT, E]), ALU.is_equal).then_inc(f_ab2, 1)
                ve.wait_ge(f_ab2, 3 * g + 3)
                nc.vector.tensor_tensor(chosen[:, 0, :, :], oh[:, 0, :, :], oh[:, 1, :, :], ALU.add).then_inc(f_dve, 1)
                ve.wait_ge(f_dve, 15 * g + 11)
                nc.vector.tensor_copy(chosen[:, 1, 1, :], chosen[:, 0, 0, :]).then_inc(f_dve, 1)
                for j in range(2, GT + 1):
                    ve.wait_ge(f_dve, 15 * g + (10 + j))
                    nc.vector.tensor_tensor(chosen[:, 1, j, :] if j < GT else total[:, :], chosen[:, 1, j - 1, :], chosen[:, 0, j - 1, :],
                                            ALU.add).then_inc(f_dve, 1)
                ve.wait_ge(f_rank, g + 1)
                rk = ps[7][:, 128:128 + GT * E].rearrange("p (j e) -> p j e", j=GT)
                nc.vector.tensor_tensor(rank, rk, run[:, par, :].unsqueeze(1).to_broadcast([P, GT, E]), ALU.add).then_inc(f_c, 1)
                nc.vector.tensor_tensor(run[:, 1 - par, :], ps[7][:, 256:256 + E], run[:, par, :], ALU.add).then_inc(f_c, 1)
                ve.wait_ge(f_c, 6 * g + 2)
                nc.vector.tensor_tensor(rank, rank, ebase[:, :].unsqueeze(1).to_broadcast([P, GT, E]), ALU.add).then_inc(f_c, 1)
                ve.wait_ge(f_c, 6 * g + 3)
                for c in range(2):
                    nc.vector.tensor_tensor(hit[:, c, :, :], oh[:, c, :, :], rank, ALU.mult).then_inc(f_c, 1)
                ve.wait_ge(f_c, 6 * g + 5)
                nc.vector.tensor_reduce(slotf, hit, AX.X, ALU.add).then_inc(f_c, 1)
                ve.wait_ge(f_c, 6 * g + 6)
                nc.vector.tensor_copy(slot[:, par, :, :], slotf).then_inc(f_slot, 1)
                ve.wait_ge(fy_done, g + 1)
                xg = x_res[:, GT * g:GT * g + GT, :] if isinstance(g, int) else x_res[:, bass.ds(GT * g, GT), :]
                xg = xg.rearrange("p j d -> p (j d)")
                nc.vector.scalar_tensor_tensor(y8, ps[4][:, :], tg01[:, 0:1], xg, ALU.mult, ALU.add).then_inc(f_x2, 1)
                ve.wait_ge(f_x2, 2 * g + 1)
                nc.vector.tensor_tensor(xg.rearrange("p (j d) -> p j d", j=GT), y8.rearrange("p (j d) -> p j d", j=GT),
                                        tgbs2[:, :].unsqueeze(1).to_broadcast([P, GT, D]), ALU.add).then_inc(f_x2, 1)

            norm2(0, 0)
            groups(ve, group)
            ve.wait_ge(f_c, 6 * GROUPS)

            chain = [0]

            def link(ins):
                chain[0] += 1
                ins.then_inc(sc_step, 1)
                ve.wait_ge(sc_step, chain[0])

            cnt = run[:, GROUPS % 2, :]
            link(nc.vector.tensor_copy(cnt_i[:, :], cnt))
            link(nc.vector.tensor_tensor(big[:, 1:E, :], big[:, 0, :].unsqueeze(1).to_broadcast([P, E - 1, 32]),
                                         cnt[:, 1:E].unsqueeze(2).to_broadcast([P, E - 1, 32]), ALU.is_lt))
            link(nc.vector.tensor_scalar(big[:, 0, :], big[:, 0, :], cnt[:, 0:1], None, ALU.is_lt))
            link(nc.vector.tensor_reduce(nt[:, :], big[:, :, :], AX.X, ALU.add))
            link(nc.vector.tensor_copy(cum[:, 0, :], nt[:, :]))
            src = 0
            for sh in (1, 2, 4):
                link(nc.vector.tensor_copy(cum[:, 1 - src, 0:sh], cum[:, src, 0:sh]))
                link(nc.vector.tensor_tensor(cum[:, 1 - src, sh:E], cum[:, src, sh:E], cum[:, src, 0:E - sh], ALU.add))
                src = 1 - src
            link(nc.vector.tensor_tensor(past[:, :, :], tile_n[:, :].unsqueeze(2).to_broadcast([P, NT, E]),
                                         cum[:, src, :].unsqueeze(1).to_broadcast([P, NT, E]), ALU.is_ge))
            link(nc.vector.tensor_reduce(sched[:, 0, :], past[:, :, :], AX.X, ALU.add))
            link(nc.vector.tensor_tensor(past[:, :, :], past[:, :, :], nt[:, :].unsqueeze(1).to_broadcast([P, NT, E]), ALU.mult))
            link(nc.vector.tensor_reduce(sched[:, 1, :], past[:, :, :], AX.X, ALU.add))
            link(nc.vector.tensor_tensor(sched[:, 1, :], tile_n[:, :], sched[:, 1, :], ALU.subtract))
            link(nc.vector.tensor_scalar(sched[:, 2, :], sched[:, 0, :], float(REGION), None, ALU.mult))
            link(nc.vector.tensor_scalar(sched[:, 1, :], sched[:, 1, :], float(P), None, ALU.mult))
            link(nc.vector.tensor_tensor(sched[:, 1, :], sched[:, 1, :], sched[:, 2, :], ALU.add))
            link(nc.vector.tensor_scalar(sched[:, 0, :], sched[:, 0, :], float(E - 1), None, ALU.min))
            nc.vector.tensor_copy(sched_i[:, :, :], sched[:, 0:2, :]).then_inc(sched_ready, 1)

            def row_step(n, q, k):
                par = q % 2
                if is_row_tile(k + 2):
                    b4 = (q + 2) % 4
                    ve.wait_ge(r_in[b4], 4 * (n + (2 - b4)) + 16)
                    if k + 2 >= 4:
                        ve.wait_ge(r_sent[b4], 4 * (n + (2 - b4)))
                    nc.vector.tensor_copy(xs_ix[:, b4:b4 + 1], xs_in[:, b4, D:ROW].bitcast(I32)).then_inc(r_ix, 1)
                if is_row_tile(k):
                    if k >= 2:
                        ve.wait_ge(r_y, n - 1)
                    ve.wait_ge(r_ta, n + 1)
                    nc.vector.tensor_copy(hid_T[:, par, :], ps[2 + par][:, :]).then_inc(r_aT, 1)
                if is_row_tile(k + 2):
                    ve.wait_ge(r_hi, n + 3)
                    nc.vector.tensor_tensor(xs_lo[:, par, :], ps[6 + par][:, 0:P], xs_hi[:, par, :].bitcast(F32), ALU.subtract).then_inc(r_lo, 1)

            row_steps(ve, row_step)

            for g in range(GROUPS):
                ve.wait_ge(o_in[g % 2], 32 * (g // 2 + 1))
                for j in range(GT):
                    t = GT * g + j
                    nc.vector.scalar_tensor_tensor(x_res[:, t, :], y_in[:, g % 2, 0, j, :], wtok[:, t, 0:1], x_res[:, t, :],
                                                   ALU.mult, ALU.add).then_inc(o_a, 1)
                for j in range(GT):
                    t = GT * g + j
                    ve.wait_ge(o_a, t + 1)
                    nc.vector.scalar_tensor_tensor(x_res[:, t, :], y_in[:, g % 2, 1, j, :], wtok[:, t, 1:2], x_res[:, t, :],
                                                   ALU.mult, ALU.add).then_inc(o_b, 1)

        @block.tensor
        def _(pe):
            pe.wait_ge(ident_ready, 1)
            pe.wait_ge(w_ready, 1)
            pe.wait_ge(wu_in, 16)

            def project(out_bank, par, src, w, cols):
                nc.tensor.matmul(out_bank, xc_hi[:, par, src, :], w_hi[:, w, cols], start=True, stop=False)
                nc.tensor.matmul(out_bank, xc_hi[:, par, src, :], w_lo[:, w, cols], start=False, stop=False)
                return nc.tensor.matmul(out_bank, xc_lo[:, par, src, :], w_hi[:, w, cols], start=False, stop=True)

            def step(s, par, k):
                cols = (slice(0, 512), slice(512, 1024))
                if has(k):
                    pe.wait_ge(qn_ready, 4 * s + 4)
                    if has(k + 1):
                        pe.wait_ge(xlo_ready, s + 2)
                    if k >= 2:
                        pe.wait_ge(o_ready, 2 * s - 2)
                        pe.wait_ge(y_read, s - 1)
                    for n, (done, free) in enumerate(((qt_done, None), (kt_done, qT_ready))):
                        for j in range(2):
                            if free is not None:
                                pe.wait_ge(free, 2 * s + (j + 1))
                            for a in range(4):
                                c0 = (4 * j + a) * P
                                last = nc.tensor.transpose(ps[6 + j][:, a * P:(a + 1) * P], qk_n[:, n, c0:c0 + P], ident[:, :])
                            last.then_inc(done, 1)
                if has(k + 1):
                    if not has(k):
                        pe.wait_ge(xlo_ready, s + 2)
                    opar = 1 - par
                    for j in range(4):
                        project(ps[j][:, :], opar, j // 2, j // 2, cols[j % 2]).then_inc(proj_done, 1)
                if has(k):
                    if k >= 1:
                        pe.wait_ge(sub_ready, 2 * s)
                    for j in range(2):
                        project(ps[4 + j][:, :], par, 1, 2, cols[j]).then_inc(v_done, 1)
                if has(k - 1):
                    pe.wait_ge(p_ready, s)
                    for j in range(2):
                        if has(k):
                            pe.wait_ge(kT_ready, 2 * s + (j + 1))
                        elif j == 0:
                            pe.wait_ge(o_ready, 2 * s - 2)
                            pe.wait_ge(y_read, s - 1)
                        for a in range(4):
                            last = nc.tensor.transpose(ps[6 + j][:, a * P:(a + 1) * P],
                                                       prob[:, 4 * j + a, :, :].rearrange("p b n -> p (b n)"), ident[:, :])
                        last.then_inc(pt_done, 1)
                if has(k):
                    wait_apart(pe, kT_ready, 2 * s + 2)
                    pe.wait_ge(qT_ready, 2 * s + 2)
                    for b in range(2):
                        wait_apart(pe, v_ready, 2 * s + (b + 1))
                        for p in range(PAIRS):
                            for h in range(2):
                                rows = slice(h * HD, (h + 1) * HD)
                                last = nc.tensor.matmul(ps[4 + b][rows, p * S:(p + 1) * S], qk_T[rows, 0, p, b * S:(b + 1) * S],
                                                        qk_T[rows, 1, p, b * S:(b + 1) * S], start=True, stop=True)
                        last.then_inc(s_done, 1)
                if has(k - 1):
                    wait_apart(pe, pt0_ready, s)
                    pe.wait_ge(pt1_ready, s)
                    vpar = 1 - par
                    for b in range(2):
                        rows = slice(b * S, (b + 1) * S)
                        for p in range(PAIRS):
                            for h in range(2):
                                last = nc.tensor.matmul(ps[6 + b][h * HD:(h + 1) * HD, p * S:(p + 1) * S],
                                                        v_sb[rows, vpar, (2 * p + h) * HD:(2 * p + h + 1) * HD],
                                                        prob_T[rows, p, h * S:(h + 1) * S], start=True, stop=True)
                        last.then_inc(o_done, 1)
                if has(k + 2):
                    pe.wait_ge(xn_ready, s + 3)
                    pe.wait_ge(c_loaded[par], 8 * (s + 2 - par) + 16)
                    if has(k - 1):
                        pe.wait_ge(o_ready, 2 * s - 1)
                    elif has(k):
                        pe.wait_ge(kT_ready, 2 * s + 2)
                    elif has(k + 1):
                        pe.wait_ge(xlo_ready, s + 2)
                    nc.tensor.transpose(ps[6][:, 0:P], xn[:, :], ident[:, :])
                    nc.tensor.transpose(ps[6][:, P:2 * P], c_in[:, par, :], ident[:, :]).then_inc(xt_done, 1)
                if has(k - 1):
                    pe.wait_ge(o_ready, 2 * s)
                    for p in range(PAIRS):
                        last = nc.tensor.matmul(ps[7][:, 0:D], o_T[:, p, :, :].rearrange("p b n -> p (b n)"), wu_sb[:, p, :],
                                                start=(p == 0), stop=(p == PAIRS - 1))
                    last.then_inc(y_done, 1)

            steps(pe, step)

            pe.wait_ge(ffw_ready, 4)
            pe.wait_ge(y_read, TILES)
            def group(g, par, last):
                pe.wait_ge(f_xn, GT * g + GT)
                for j in range(GT):
                    last_ = nc.tensor.transpose(ps[6][:, j * P:(j + 1) * P], rows[:, par, 0, j, 0:D], ident[:, :])
                last_.then_inc(f_t, 1)
                pe.wait_ge(f_lo, g + 1)
                for j in range(GT):
                    for n, (a, w) in enumerate(((gT_lo, wg_lo), (gT_lo, wg_hi), (gT_hi, wg_lo), (gT_hi, wg_hi))):
                        last_ = nc.tensor.matmul(ps[7][:, j * E:(j + 1) * E], a[:, j * P:(j + 1) * P], w[:, :], start=(n == 0), stop=(n == 3))
                last_.then_inc(f_lg, 1)
                for c in range(CH):
                    fs = slice(c * P, (c + 1) * P)
                    nc.tensor.matmul(ps[c][:, :], w1_hi[:, E, fs], gT_hi, start=True, stop=False)
                    nc.tensor.matmul(ps[c][:, :], w1_hi[:, E, fs], gT_lo, start=False, stop=False)
                    nc.tensor.matmul(ps[c][:, :], w1_lo[:, E, fs], gT_hi, start=False, stop=True).then_inc(h_done, 1)
                for c in range(CH):
                    pe.wait_ge(act_ready, CH * g + (c + 1))
                for j in range(GT):
                    for c in range(CH):
                        last_ = nc.tensor.matmul(ps[4][:, j * D:(j + 1) * D], act[:, c, j * P:(j + 1) * P], w2_sb[:, E, c, :],
                                                 start=(c == 0), stop=(c == CH - 1))
                last_.then_inc(fy_done, 1)
                pe.wait_ge(f_dve, 15 * g + 15)
                for j in range(GT):
                    out_j = ps[7][:, 128 + j * E:128 + (j + 1) * E]
                    nc.tensor.matmul(out_j, before[:, :], chosen[:, 0, j, :], start=True, stop=(j == 0))
                    if j > 0:
                        nc.tensor.matmul(out_j, ones_b[:, :], chosen[:, 1, j, :], start=False, stop=True)
                nc.tensor.matmul(ps[7][:, 256:256 + E], ones_b[:, :], total[:, :], start=True, stop=True).then_inc(f_rank, 1)

            groups(pe, group)
            pe.wait_ge(sched_ready, 1)
            pe.wait_ge(bias_ready, 96)
            pe.wait_ge(rows3_ready, 3)

            def row_step(n, q, k):
                par = q % 2
                if is_row_tile(k + 1):
                    e = pe.value_load(tile_of_sched(0, n + 1), min_val=0, max_val=E - 1)
                    pe.wait_ge(r_lo, n + 2)
                    if k + 1 >= 2:
                        pe.wait_ge(r_act, n)
                    h = ps[1 - par][:, :]

                    def of(w):
                        return w[:, bass.ds(e, 1), :].rearrange("p a n -> p (a n)")

                    nc.tensor.matmul(h, rows3[:, :], of(b1_parts), start=True, stop=False)
                    nc.tensor.matmul(h, xs_hi[:, 1 - par, :], of(w1_hi), start=False, stop=False)
                    nc.tensor.matmul(h, xs_hi[:, 1 - par, :], of(w1_lo), start=False, stop=False)
                    nc.tensor.matmul(h, xs_lo[:, 1 - par, :], of(w1_hi), start=False, stop=True).then_inc(r_h, 1)
                if is_row_tile(k + 2):
                    b4 = (q + 2) % 4
                    pe.wait_ge(r_in[b4], 4 * (n + (2 - b4)) + 16)
                    if k + 2 >= 2:
                        pe.wait_ge(r_lo, n + 1)
                    nc.tensor.transpose(ps[6 + par][:, 0:P], xs_in[:, b4, 0:D], ident[:, :]).then_inc(r_t, 1)
                if is_row_tile(k - 1):
                    e = pe.value_load(tile_of_sched(0, n - 1), min_val=0, max_val=E - 1)
                    pe.wait_ge(r_aT, n)
                    if k - 1 >= 2:
                        pe.wait_ge(r_yb, n - 2)
                    y = ps[4 + (1 - par)][:, 0:D]
                    nc.tensor.matmul(y, rows3[:, :], b2_parts[:, bass.ds(e, 1), :].rearrange("p a n -> p (a n)"), start=True, stop=False)
                    w2e = w2_sb[:, bass.ds(e, 1), :, :].rearrange("p a c n -> p (a c) n")
                    for c in range(CH):
                        last_ = nc.tensor.matmul(y, hid_T[:, 1 - par, c * P:(c + 1) * P], w2e[:, c, :], start=False, stop=(c == CH - 1))
                    last_.then_inc(r_y, 1)
                if is_row_tile(k):
                    pe.wait_ge(r_act, n + 1)
                    if k >= 2:
                        pe.wait_ge(r_aT, n - 1)
                    for c in range(CH):
                        last_ = nc.tensor.transpose(ps[2 + par][:, c * P:(c + 1) * P], hid[:, par, c * P:(c + 1) * P], ident[:, :])
                    last_.then_inc(r_ta, 1)

            row_steps(pe, row_step)


_INS = ['x', 'ctx_1024', 'g_xattn', 'g_ffn', 'L0_xattn_Wq', 'L0_xattn_Wk', 'L0_xattn_Wv', 'L0_xattn_Wu', 'L0_xattn_bu',
        'L0_xattn_qn_w', 'L0_xattn_qn_b', 'L0_xattn_kn_w', 'L0_xattn_kn_b', 'L0_ffn_Wg', 'L0_ffn_W1', 'L0_ffn_b1',
        'L0_ffn_W2', 'L0_ffn_b2', 'L0_ffn_Ws1', 'L0_ffn_bs1', 'L0_ffn_Ws2', 'L0_ffn_bs2']
_TRANSPOSED = ('L0_xattn_Wq', 'L0_xattn_Wk', 'L0_xattn_Wv', 'L0_xattn_Wu')
_BY_HIDDEN_UNIT = ('L0_ffn_bs1',)


def kernel(**inputs):
    import numpy as np
    import concourse.bacc as bacc
    from concourse.bass_utils import run_bass_kernel_spmd

    nc = bacc.Bacc("TRN2", target_bir_lowering=False, num_devices=1)
    arrays, args = {}, []
    for name in _INS:
        a = np.asarray(inputs[name])
        if name in _TRANSPOSED:
            a = a.T
        if name in _BY_HIDDEN_UNIT:
            a = a.reshape(-1, P).T
        a = np.ascontiguousarray(a)
        arrays[f"in_{name}"] = a
        args.append(nc.dram_tensor(f"in_{name}", a.shape, mybir.dt.from_np(a.dtype), kind="ExternalInput").ap())
    args.append(nc.dram_tensor("out_x", [B, S, D], F32, kind="ExternalOutput").ap())
    flamingo_block(nc, *args)
    r = run_bass_kernel_spmd(nc, [arrays], core_ids=[0])
    return r.results[0]["out_x"]
```

```python
import concourse.bass as bass
from concourse import mybir
from contextlib import ExitStack

F32 = mybir.dt.float32
F32R = mybir.dt.float32r
BF16 = mybir.dt.bfloat16
I32 = mybir.dt.int32
U32 = mybir.dt.uint32
ALU = mybir.AluOpType
ACT = mybir.ActivationFunctionType
AX = mybir.AxisListType

P = 128
B, S, D = 64, 64, 128
HEADS, HD = 16, 64
INNER = HEADS * HD
TOKENS = B * S
TILES = TOKENS // P
PAIRS = HEADS // 2
E, FF = 8, 512
NX = E + 1
CH = FF // P
GT = 4
GROUPS = TILES // GT
GN = GT * P
ROW = D + 1
REGION = TOKENS + P
SPARE = 8
NT = 72
LN_EPS = 1e-5
TOPK_EPS = 1e-9
SHARED = 0.1


def flamingo_block(nc, x, ctx, g_xattn, g_ffn, wqT, wkT, wvT, wuT, bu, qn_w, qn_b, kn_w, kn_b,
                   wg, w1, b1, w2, b2, ws1, bs1, ws2, bs2, out):
    x_v = x.rearrange("b s d -> (b s) d").rearrange("(t p) d -> p t d", p=P)
    ctx_v = ctx.rearrange("b s d -> (b s) d").rearrange("(t p) d -> p t d", p=P)
    out_v = out.rearrange("b s d -> (b s) d").rearrange("(t p) d -> p t d", p=P)

    with ExitStack() as stack:
        def sb(name, shape, dt=F32):
            return stack.enter_context(nc.sbuf_tensor(name, shape, dt))

        def bank(name):
            return stack.enter_context(nc.psum_tensor(name, [P, 512], F32))

        def sem(name):
            return stack.enter_context(nc.semaphore(name))

        x_res = sb("x_res", [P, TILES, D])
        c_in = sb("c_in", [P, 2, D])
        xn = sb("xn", [P, D])
        xc_hi = sb("xc_hi", [P, 2, 2, P], F32R)
        xc_lo = sb("xc_lo", [P, 2, 2, P], F32R)
        w_raw = sb("w_raw", [P, 3, INNER])
        w_hi = sb("w_hi", [P, 3, INNER], F32R)
        w_lo = sb("w_lo", [P, 3, INNER], F32R)
        w_mean = sb("w_mean", [P, 2, HEADS])
        wu_sb = sb("wu_sb", [P, PAIRS, D])
        wide = sb("wide", [P, 4, INNER])
        sq = wide[:, 0:2, :]
        ss = sb("ss", [P, 2, HEADS])
        rstd = sb("rstd", [P, 2, HEADS])
        var_eps = sb("var_eps", [P, 2, HEADS])
        qk_n = wide[:, 2:4, :]
        qk_T = sb("qk_T", [P, 2, PAIRS, P])
        v_sb = sb("v_sb", [P, 2, INNER])
        prob = sb("prob", [P, PAIRS, 2, S])
        spo = sb("spo", [P, 2 * E * (D + 1)])
        prob_T = spo[:, 0:INNER].rearrange("p (a n) -> p a n", a=PAIRS)
        o_T = spo[:, INNER:2 * INNER].rearrange("p (a b n) -> p a b n", a=PAIRS, b=2)
        mx = sb("mx", [P, 2, PAIRS])
        sm = sb("sm", [P, PAIRS * 2])
        rinv = sb("rinv", [P, PAIRS * 2])
        y_tmp = sb("y_tmp", [P, D])
        lnw = sb("lnw", [P, 4])
        gates = sb("gates", [P, 2])
        tg = sb("tg", [P, 2])
        bu_b = sb("bu_b", [P, D])
        tgbu = sb("tgbu", [P, D])
        ident = sb("ident", [P, P])
        expo = sb("expo", [P, 2, HEADS])
        eps = sb("eps", [P, 2, HEADS])
        bn6 = sb("bn6", [P, 6])
        mv = sb("mv", [P, 2])
        xv_eps = sb("xv_eps", [P, 1])
        x_rstd = sb("x_rstd", [P, 1])
        wg_raw = sb("wg_raw", [P, E])
        wg_hi = sb("wg_hi", [P, E], F32R)
        wg_lo = sb("wg_lo", [P, E], F32R)
        w1_raw = sb("w1_raw", [P, NX, FF])
        w1_hi = sb("w1_hi", [P, NX, FF], F32R)
        w1_lo = sb("w1_lo", [P, NX, FF], F32R)
        w2_sb = sb("w2_sb", [P, NX, CH, D])
        bs1_sb = sb("bs1_sb", [P, CH])
        late = w_raw[:, :, :].rearrange("p a n -> p (a n)")
        BC = E * (FF + D) // P
        b_raw = sb("b_raw", [P, BC])
        b_cols = sb("b_cols", [P, 3, BC], BF16)
        b1_parts = sb("b1_parts", [P, E, FF], BF16)
        b2_parts = sb("b2_parts", [P, E, D], BF16)
        rows = late[:, 0:2 * 2 * GT * ROW].rearrange("p (u c j n) -> p u c j n", u=2, c=2, j=GT)
        o = 2 * 2 * GT * ROW
        router = {}
        for name, width in (("lg", GT * E), ("gm", GT), ("gs", GT), ("gtop", GT * 8), ("gidf", GT * 2), ("gw", GT * 2),
                            ("oh", 2 * GT * E), ("rank", GT * E), ("hit", 2 * GT * E), ("slotf", 2 * GT)):
            router[name] = late[:, o:o + width]
            o += width
        assert o <= 3 * INNER
        gp = router["lg"].rearrange("p (j e) -> p j e", j=GT)
        gm, gs = router["gm"], router["gs"]
        gtop = router["gtop"].rearrange("p (j e) -> p j e", j=GT)
        gidf = router["gidf"].rearrange("p (j e) -> p j e", j=GT)
        gw = router["gw"].rearrange("p (j e) -> p j e", j=GT)
        oh = router["oh"].rearrange("p (c j e) -> p c j e", c=2, j=GT)
        rank = router["rank"].rearrange("p (j e) -> p j e", j=GT)
        hit = router["hit"].rearrange("p (c j e) -> p c j e", c=2, j=GT)
        slotf = router["slotf"].rearrange("p (c j) -> p c j", c=2)
        y8 = prob[:, 0:4, :, :].rearrange("p a b n -> p (a b n)")
        gT = sb("gT", [P, 2, GN], F32R)
        gT_hi, gT_lo = gT[:, 0, :], gT[:, 1, :]
        act = wide[:, 0:2, :].rearrange("p a n -> p (a n)").rearrange("p (c n) -> p c n", c=CH)
        bn6_2 = sb("bn6_2", [P, 6])
        mv_tile = sb("mv_tile", [P, 2])
        mv_2 = sb("mv_2", [P, TILES, 2])
        ve_2 = sb("ve_2", [P, TILES])
        rstd_2 = sb("rstd_2", [P, TILES])
        normed = wide[:, 2:4, :].rearrange("p a (j n) -> p a j n", n=D)[:, :, 0:GT, :]
        gidx = sb("gidx", [P, GT, 8], U32)
        chosen = sb("chosen", [P, 2, GT, E], BF16)
        total = sb("total", [P, E], BF16)
        run = sb("run", [P, 2, E])
        slot = sb("slot", [P, 2, 2, GT], I32)
        wtok = sb("wtok", [P, TILES, 2])
        iot = sb("iot", [P, E])
        iot_i = sb("iot_i", [P, E], I32)
        ebase = sb("ebase", [P, E])
        ebase_i = sb("ebase_i", [P, E], I32)
        tok_i = sb("tok_i", [P, 2, TILES], I32)
        before = sb("before", [P, P], BF16)
        ones_b = sb("ones_b", [P, P], BF16)
        rows3 = sb("rows3", [P, P], BF16)
        tgbs2 = sb("tgbs2", [P, D])
        tg01 = sb("tg01", [P, 1])
        nt = sb("nt", [P, E])
        big = sb("big", [P, E, 32])
        cum = sb("cum", [P, 2, E])
        tile_n = sb("tile_n", [P, NT])
        past = sb("past", [P, NT, E])
        sched = sb("sched", [P, 3, NT])
        sched_i = sb("sched_i", [P, 2, NT], I32)
        cnt_i = sb("cnt_i", [P, E], I32)
        i32s = sb("i32s", [P, 256], I32)
        pad = spo[:, :].rearrange("p (k n) -> p k n", n=ROW)
        xs_in = v_sb[:, :, :].rearrange("p a n -> p (a n)")[:, 0:4 * ROW].rearrange("p (k n) -> p k n", k=4)
        xs_hi = sb("xs_hi", [P, 2, P], F32R)
        xs_lo = sb("xs_lo", [P, 2, P], F32R)
        xs_ix = sb("xs_ix", [P, 4], I32)
        hid = qk_T[:, :, :, :].rearrange("p a b n -> p (a b n)")[:, 0:2 * FF].rearrange("p (a n) -> p a n", a=2)
        hid_T = qk_T[:, :, :, :].rearrange("p a b n -> p (a b n)")[:, 2 * FF:4 * FF].rearrange("p (a n) -> p a n", a=2)
        yb = o_T[:, :, :, :].rearrange("p a b n -> p (a b n)")[:, 0:4 * D].rearrange("p (k n) -> p k n", k=4)
        y_in = [a[:, 0:4 * 2 * GN].rearrange("p (u c j n) -> p u c j n", u=4, c=2, j=GT)[:, u, :, :, :]
                for a in (wide[:, :, :].rearrange("p a n -> p (a n)"), w1_raw[:, :, :].rearrange("p e n -> p (e n)")) for u in range(4)]

        ps = [bank(f"ps{i}") for i in range(8)]

        const_in, wu_in, ffw_in, w2_in = sem("const_in"), sem("wu_in"), sem("ffw_in"), sem("w2_in")
        w_in = [sem("wq_in"), sem("wk_in"), sem("wv_in")]
        x_first, x_in = sem("x_first"), sem("x_in")
        c_loaded = [sem("c_loaded0"), sem("c_loaded1")]
        ones_ready, ident_ready, expo_ready = sem("ones_ready"), sem("ident_ready"), sem("expo_ready")
        w_step, w_centred, w_hi_ready, w_ready, wv_ready = (sem(n) for n in ("w_step", "w_centred", "w_hi_ready", "w_ready", "wv_ready"))
        tanh_ready, tgbu_ready = sem("tanh_ready"), sem("tgbu_ready")
        bn_done, mv_ready, xve_ready, xrs_ready, xn_ready = (sem(n) for n in ("bn_done", "mv_ready", "xve_ready", "xrs_ready", "xn_ready"))
        xt_done, xhi_ready, xlo_ready = sem("xt_done"), sem("xhi_ready"), sem("xlo_ready")
        proj_done, sq_ready, ss_ready, ve_ready, rstd_ready, qn_ready = (
            sem(n) for n in ("proj_done", "sq_ready", "ss_ready", "ve_ready", "rstd_ready", "qn_ready"))
        qt_done, kt_done, qT_ready, kT_ready = sem("qt_done"), sem("kt_done"), sem("qT_ready"), sem("kT_ready")
        v_done, v_ready = sem("v_done"), sem("v_ready")
        s_done, mx_ready, sub_ready, exp_ready, sum_ready, rinv_ready, p_ready = (
            sem(n) for n in ("s_done", "mx_ready", "sub_ready", "exp_ready", "sum_ready", "rinv_ready", "p_ready"))
        pt_done, pt_ready = sem("pt_done"), sem("pt_ready")
        o_done, o_ready, y_done, y_read, x1_ready = (sem(n) for n in ("o_done", "o_ready", "y_done", "y_read", "x1_ready"))
        agg2_done = sem("agg2_done")
        bn2_done, mv2_ready, ve2_ready, rstd2_ready = (sem(n) for n in ("bn2_done", "mv2_ready", "ve2_ready", "rstd2_ready"))
        f_xn, f_row = sem("f_xn"), sem("f_row")
        f_t, f_hi, f_lo, f_lg, f_dve, f_exp, f_ab = (sem(n) for n in ("f_t", "f_hi", "f_lo", "f_lg", "f_dve", "f_exp", "f_ab"))
        f_hot, f_c, rows3_ready = sem("f_hot"), sem("f_c"), sem("rows3_ready")
        f_rank, f_slot, h_done, act_ready, fy_done, f_x2 = (
            sem(n) for n in ("f_rank", "f_slot", "h_done", "act_ready", "fy_done", "f_x2"))
        f_sent = [sem("f_sent0"), sem("f_sent1")]
        w1hi_ready = sem("w1hi_ready")
        ffw_ready, bias_in, bias_prep, bias_ready, gp_const, pad_ready, run0 = (
            sem(n) for n in ("ffw_ready", "bias_in", "bias_prep", "bias_ready", "gp_const", "pad_ready", "run0"))
        sc_step, cnt_ready, sched_ready, padded = sem("sc_step"), sem("cnt_ready"), sem("sched_ready"), sem("padded")
        r_in = [sem(f"r_in{k}") for k in range(4)]
        r_t, r_hi, r_lo, r_ix, r_h, r_act, r_ta, r_aT, r_y, r_yb = (
            sem(n) for n in ("r_t", "r_hi", "r_lo", "r_ix", "r_h", "r_act", "r_ta", "r_aT", "r_y", "r_yb"))
        r_sent = [sem(f"r_sent{k}") for k in range(4)]
        o_in, o_a, o_b = [sem(f"o_in{g}") for g in range(GROUPS)], sem("o_a"), sem("o_b")
        o_w = sem("o_w")
        o_stored = sem("o_stored")

        routed = nc.dram_tensor("routed", [E * REGION + SPARE * P, ROW], F32, kind="Internal").ap()
        bias1 = nc.dram_tensor("bias1", [3, E * FF], BF16, kind="Internal").ap()
        bias2 = nc.dram_tensor("bias2", [3, E * D], BF16, kind="Internal").ap()
        results = nc.dram_tensor("results", [2 * TOKENS + 2 * E * P, D], F32, kind="Internal").ap()

        block = stack.enter_context(nc.Block())

        STEADY = range(3, TILES - 3)

        def steps(eng, step):
            for s in range(-3, STEADY.start):
                step(s, s % 2, s)
            with eng.Fori(0, len(STEADY) // 2) as i:
                for half in range(2):
                    step(2 * i + (STEADY.start + half), (STEADY.start + half) % 2, STEADY.start)
            for s in range(STEADY.stop, TILES + 2):
                step(s, s % 2, s)

        W1_COLS = NX * FF
        W1_SLICE = W1_COLS // len(STEADY) // 32 * 32
        W1_STEPS = range(STEADY.start, STEADY.stop + 1)
        w1_raw_cols, w1_hi_cols, w1_lo_cols = (w[:, :, :].rearrange("p e f -> p (e f)") for w in (w1_raw, w1_hi, w1_lo))

        def w1_slices(s, k):
            if k == STEADY.stop:
                return [slice(W1_SLICE * len(STEADY), W1_COLS)]
            return [bass.ds(W1_SLICE * s - W1_SLICE * STEADY.start, W1_SLICE)]

        def wait_apart(eng, semaphore, value, *more):
            waits = [(semaphore, value), *more]
            for _, count in waits:
                if not isinstance(count, int):
                    eng.compute_val(count)
            eng.wait_ge(ident_ready, 1)
            for which, count in waits:
                eng.wait_ge(which, count)

        def has(s):
            return 0 <= s < TILES

        def groups(eng, group):
            for g in range(2):
                group(g, g, False)
            with eng.Fori(0, GROUPS // 2 - 2) as i:
                for half in range(2):
                    group(2 * i + (2 + half), half, False)
            for g in range(GROUPS - 2, GROUPS):
                group(g, g % 2, g == GROUPS - 1)

        ROUTED = range(4, NT - 4)
        RU = 16

        def row_steps(eng, step):
            for n in range(-2, ROUTED.start):
                step(n, n % 4, n, n + 2)
            with eng.Fori(0, len(ROUTED) // RU) as i:
                for u in range(RU):
                    step(RU * i + (ROUTED.start + u), (ROUTED.start + u) % 4, ROUTED.start, u)
            for n in range(ROUTED.stop, NT + 1):
                step(n, n % 4, n, n - ROUTED.stop)

        def tile_of_sched(what, n):
            return sched_i[0:1, what, n:n + 1] if isinstance(n, int) else sched_i[0:1, what, bass.ds(n, 1)]

        def is_row_tile(n):
            return 0 <= n < NT

        def tile_of(a, t):
            return a[:, t, :] if isinstance(t, int) else a[:, bass.ds(t, 1), :].rearrange("p a d -> p (a d)")

        def col_of(a, t):
            return a[:, t:t + 1] if isinstance(t, int) else a[:, bass.ds(t, 1)]

        @block.sync
        def _(sp):
            first = TILES // 8
            sp.dma_start(x_res[:, 0:first, :], x_v[:, 0:first, :]).then_inc(x_first, 16)
            for n, w in enumerate((wqT, wkT, wvT)):
                sp.dma_start(w_raw[:, n, :], w).then_inc(w_in[n], 16)
                if n < 2:
                    sp.dma_start(c_in[:, n, :], ctx_v[:, n, :]).then_inc(c_loaded[n], 16)
            for n, src in enumerate((g_xattn, g_ffn)):
                sp.dma_start(gates[:, n:n + 1], src.rearrange("(a n) -> a n", a=1).partition_broadcast(P).rearrange("p a n -> p (a n)")).then_inc(const_in, 16)
            sp.dma_start(bu_b[:, :], bu.rearrange("(a n) -> a n", a=1).partition_broadcast(P).rearrange("p a n -> p (a n)")).then_inc(const_in, 16)
            for n, src in enumerate((qn_w, qn_b, kn_w, kn_b)):
                for h in range(2):
                    sp.dma_start(lnw[h * HD:(h + 1) * HD, n:n + 1], src.rearrange("(p a) -> p a", a=1)).then_inc(const_in, 16)
            sp.dma_start(tgbs2[:, :], bs2.rearrange("(a n) -> a n", a=1).partition_broadcast(P).rearrange("p a n -> p (a n)")).then_inc(const_in, 16)
            sp.dma_start(x_res[:, first:TILES, :], x_v[:, first:TILES, :]).then_inc(x_in, 16)
            sp.dma_start(wu_sb[:, :, :], wuT.rearrange("(c p) n -> p c n", p=P)).then_inc(wu_in, 16)
            with sp.Fori(0, TILES // 2 - 1) as i:
                for half in range(2):
                    sp.compute_val(2 * i + (half + 2))
                    wait_apart(sp, xt_done, 2 * i + (half + 1))
                    sp.dma_start(c_in[:, half, :], ctx_v[:, bass.ds(2 * i + (half + 2), 1), :].rearrange("p a d -> p (a d)")
                                 ).then_inc(c_loaded[half], 16)
            sp.wait_ge(pad_ready, 2)
            sp.dma_start(routed[E * REGION:E * REGION + SPARE * P, :].rearrange("(k p) n -> p k n", p=P), pad[:, E:2 * E, :]).then_inc(padded, 16)
            sp.wait_ge(cnt_ready, 1)
            for e in range(0, E, 2):
                count = sp.value_load(cnt_i[0:1, e:e + 1], min_val=0, max_val=TOKENS)
                sp.dma_start(routed[bass.ds(count + e * REGION, P), :], pad[:, e, :]).then_inc(padded, 16)
            sp.wait_ge(sched_ready, 1)
            sp.wait_ge(padded, 16 * (E + 1))
            for par in range(2):
                sp.wait_ge(f_sent[par], 16 * GT * GROUPS)

            def step(n, q, k, u):
                if is_row_tile(k + 2):
                    row = sp.value_load(tile_of_sched(1, n + 2), min_val=0, max_val=E * REGION + SPARE * P - P)
                    if k + 2 >= 4:
                        sp.wait_ge(r_t, n - 1)
                        sp.wait_ge(r_ix, n - 1)
                    b4 = (q + 2) % 4
                    sp.dma_start(xs_in[:, b4, :], routed[bass.ds(row, P), :]).then_inc(r_in[b4], 16)

            row_steps(sp, step)

            for k in range(4):
                sp.wait_ge(r_sent[k], 16 * (NT // 4))
            res_v = results[0:2 * TOKENS, :].rearrange("(c t p) d -> p c t d", c=2, p=P)
            for g in range(GROUPS):
                for c in range(2):
                    sp.dma_start(y_in[g][:, c, :, :], res_v[:, c, GT * g:GT * g + GT, :]).then_inc(o_in[g], 16)
            for g in range(GROUPS):
                sp.wait_ge(o_b, g + 1)
                sp.dma_start(out_v[:, GT * g:GT * (g + 1), :], x_res[:, GT * g:GT * (g + 1), :]).then_inc(o_stored, 16)
            sp.wait_ge(o_stored, 16 * GROUPS)

        @block.scalar
        def _(sc):
            for n, (ready, count) in ((2, (w_in[2], 16)), (0, (w_centred, 1)), (1, (w_centred, 2))):
                sc.wait_ge(ready, count)
                nc.scalar.activation(w_hi[:, n, :], w_raw[:, n, :], ACT.Copy).then_inc(w_hi_ready, 1)
            def step(s, par, k):
                if k == 0:
                    sc.wait_ge(const_in, 12 * 16)
                    nc.scalar.activation(tg[:, :], gates[:, :], ACT.Tanh).then_inc(tanh_ready, 1)
                if k == 1:
                    sc.dma_start(wg_raw[:, :], wg).then_inc(ffw_in, 16)
                    sc.dma_start(w1_raw[:, 0:E, :], w1.rearrange("e h f -> h e f")).then_inc(ffw_in, 16)
                    sc.dma_start(w1_raw[:, E, :], ws1).then_inc(ffw_in, 16)
                if k == 2:
                    sc.dma_start(w2_sb[:, 0:E, :, :].rearrange("p e c n -> p (e c) n"),
                                 w2.rearrange("e f h -> (e f) h").rearrange("(k p) n -> p k n", p=P)).then_inc(w2_in, 16)
                    sc.dma_start(w2_sb[:, E, :, :], ws2.rearrange("(c p) n -> p c n", p=P)).then_inc(w2_in, 16)
                    sc.dma_start(bs1_sb[:, :], bs1).then_inc(w2_in, 16)
                if has(k + 2):
                    sc.wait_ge(xt_done, s + 3)
                    nc.scalar.activation(xc_hi[:, par, :, :].rearrange("p a n -> p (a n)"), ps[6][:, 0:256], ACT.Copy).then_inc(xhi_ready, 1)
                for n, (done, ready) in enumerate(((qt_done, qT_ready), (kt_done, kT_ready))):
                    if has(k):
                        for j in range(2):
                            sc.wait_ge(done, 2 * s + (j + 1))
                            nc.scalar.activation(qk_T[:, n, 4 * j:4 * j + 4, :].rearrange("p a n -> p (a n)"), ps[6 + j][:, :],
                                                 ACT.Identity, bias=lnw[:, 2 * n + 1:2 * n + 2], scale=lnw[:, 2 * n:2 * n + 1]).then_inc(ready, 1)
                    if has(k + 1):
                        if k + 1 >= 1 and n == 0:
                            sc.wait_ge(ss_ready, 2 * s + 2)
                        for j in range(2):
                            sc.wait_ge(proj_done, 4 * s + (5 + 2 * n + j))
                            nc.scalar.activation(sq[:, n, j * 512:j * 512 + 512], ps[2 * n + j][:, :],
                                                 ACT.Square, scale=HD ** -0.5).then_inc(sq_ready, 1)
                if has(k - 1):
                    for j in range(2):
                        sc.wait_ge(pt_done, 2 * s + (j - 1))
                        nc.scalar.activation(prob_T[:, 4 * j:4 * j + 4, :].rearrange("p a n -> p (a n)"), ps[6 + j][:, :],
                                             ACT.Copy).then_inc(pt_ready, 1)
                if k in W1_STEPS:
                    sc.wait_ge(ffw_in, 3 * 16)
                    for at in w1_slices(s, k):
                        nc.scalar.activation(w1_hi_cols[:, at], w1_raw_cols[:, at], ACT.Copy).then_inc(w1hi_ready, 1)

                def attention_output(b):
                    sc.wait_ge(o_done, 2 * s + (b - 1))
                    nc.scalar.activation(o_T[:, :, b, :], ps[6 + b][:, :].rearrange("p (a n) -> p a n", a=PAIRS), ACT.Copy).then_inc(o_ready, 1)

                if has(k - 1):
                    attention_output(0)
                if has(k):
                    sc.wait_ge(sub_ready, 2 * s + 2)
                    p_all = prob[:, :, :, :].rearrange("p a b n -> p (a b n)")
                    nc.scalar.activation(p_all, p_all, ACT.Exp, scale=HD ** -0.5).then_inc(exp_ready, 1)
                if has(k - 1):
                    attention_output(1)
                if has(k + 1):
                    for j in range(2):
                        sc.wait_ge(v_done, 2 * s + (j + 3))
                        nc.scalar.activation(v_sb[:, 1 - par, j * 512:(j + 1) * 512], ps[4 + j][:, :], ACT.Copy).then_inc(v_ready, 1)

            steps(sc, step)

            def hi_part(g):
                sc.wait_ge(f_t, g + 1)
                nc.scalar.activation(gT_hi, ps[6][:, :], ACT.Copy).then_inc(f_hi, 1)

            def exponentials(g):
                sc.wait_ge(f_dve, 15 * g + 2)
                nc.scalar.activation(gp, gp, ACT.Exp).then_inc(f_exp, 1)

            def group(g, par, last):
                for c in range(CH):
                    sc.wait_ge(h_done, CH * g + (c + 1))
                    nc.scalar.activation(act[:, c, :], ps[c][:, :], ACT.Silu, bias=bs1_sb[:, c:c + 1]).then_inc(act_ready, 1)
                if not last:
                    hi_part(g + 1)
                    exponentials(g + 1)

            sc.wait_ge(w2_in, 3 * 16)
            hi_part(0)
            exponentials(0)
            groups(sc, group)
            sc.wait_ge(pad_ready, 2)
            sc.wait_ge(cnt_ready, 1)
            for e in range(1, E, 2):
                count = sc.value_load(cnt_i[0:1, e:e + 1], min_val=0, max_val=TOKENS)
                sc.dma_start(routed[bass.ds(count + e * REGION, P), :], pad[:, e, :]).then_inc(padded, 16)

            def row_step(n, q, k, u):
                par = q % 2
                if is_row_tile(k + 2):
                    if k >= 0:
                        sc.wait_ge(r_h, n + 1)
                    sc.wait_ge(r_t, n + 3)
                    nc.scalar.activation(xs_hi[:, par, :], ps[6 + par][:, 0:P], ACT.Copy).then_inc(r_hi, 1)
                if is_row_tile(k + 1):
                    if k + 1 >= 2:
                        sc.wait_ge(r_ta, n)
                    sc.wait_ge(r_h, n + 2)
                    nc.scalar.activation(hid[:, 1 - par, :], ps[1 - par][:, :], ACT.Silu).then_inc(r_act, 1)
                if is_row_tile(k - 1):
                    b4 = (q - 1) % 4
                    sc.wait_ge(r_y, n)
                    if k - 1 >= 4:
                        sc.wait_ge(r_sent[b4], 4 * (n - 1 - b4) if isinstance(n, int) else 4 * (n - (1 + b4)))
                    nc.scalar.activation(yb[:, b4, :], ps[4 + (1 - par)][:, 0:D], ACT.Copy).then_inc(r_yb, 1)

            row_steps(sc, row_step)
            for g in range(GROUPS):
                sc.wait_ge(o_in[g], 32)
                for j in range(GT):
                    t = GT * g + j
                    nc.scalar.activation(y_in[g][:, 1, j, :], y_in[g][:, 1, j, :], ACT.Copy, scale=wtok[:, t, 1:2]).then_inc(o_w, 1)

        @block.gpsimd
        def _(gp_):
            nc.gpsimd.memset(ident[:, :], 0.0).then_inc(ones_ready, 1)
            gp_.wait_ge(ones_ready, 1)
            nc.gpsimd.affine_select(out=ident[:, :], in_=ident[:, :], compare_op=ALU.not_equal, fill=1.0,
                                    base=0, pattern=[[-1, P]], channel_multiplier=1).then_inc(ident_ready, 1)
            nc.gpsimd.memset(expo[:, :, :], -0.5).then_inc(expo_ready, 1)
            nc.gpsimd.memset(eps[:, :, :], LN_EPS).then_inc(expo_ready, 1)
            nc.gpsimd.iota(iot_i[:, :], pattern=[[1, E]], base=0, channel_multiplier=0).then_inc(expo_ready, 1)
            nc.gpsimd.iota(ebase_i[:, :], pattern=[[REGION, E]], base=0, channel_multiplier=0).then_inc(expo_ready, 1)
            nc.gpsimd.iota(tok_i[:, :, :], pattern=[[TOKENS, 2], [P, TILES]], base=0, channel_multiplier=1).then_inc(expo_ready, 1)
            nc.gpsimd.iota(i32s[:, 0:NT], pattern=[[1, NT]], base=0, channel_multiplier=0).then_inc(expo_ready, 1)
            nc.gpsimd.iota(i32s[:, 128:160], pattern=[[P, 32]], base=0, channel_multiplier=0).then_inc(expo_ready, 1)
            nc.gpsimd.iota(i32s[:, 200:200 + 2 * E], pattern=[[P, 2 * E]], base=2 * TOKENS, channel_multiplier=1).then_inc(expo_ready, 1)
            nc.gpsimd.memset(ones_b[:, :], 1.0).then_inc(expo_ready, 1)
            nc.gpsimd.memset(before[:, :], 1.0).then_inc(expo_ready, 1)
            gp_.wait_ge(expo_ready, 10)
            nc.gpsimd.tensor_copy(iot[:, :], iot_i[:, :]).then_inc(gp_const, 1)
            nc.gpsimd.tensor_copy(ebase[:, :], ebase_i[:, :]).then_inc(gp_const, 1)
            nc.gpsimd.tensor_copy(tile_n[:, :], i32s[:, 0:NT]).then_inc(gp_const, 1)
            nc.gpsimd.tensor_copy(big[:, 0, :], i32s[:, 128:160]).then_inc(gp_const, 1)
            nc.gpsimd.affine_select(out=before[:, :], in_=before[:, :], compare_op=ALU.is_gt, fill=0.0,
                                    base=0, pattern=[[1, P]], channel_multiplier=-1).then_inc(gp_const, 1)
            def rstd2(t):
                gp_.wait_ge(mv2_ready, t + 1)
                nc.gpsimd.tensor_tensor(col_of(ve_2, t), tile_of(mv_2, t)[:, 1:2], eps[:, 0, 0:1], ALU.add).then_inc(ve2_ready, 1)
                gp_.wait_ge(ve2_ready, t + 1)
                nc.gpsimd.tensor_tensor(col_of(rstd_2, t), col_of(ve_2, t), expo[:, 0, 0:1], ALU.pow).then_inc(rstd2_ready, 1)

            def step(s, par, k):
                if has(k + 3):
                    gp_.wait_ge(mv_ready, s + 4)
                    nc.gpsimd.tensor_tensor(xv_eps[:, :], mv[:, 1:2], eps[:, 0, 0:1], ALU.add).then_inc(xve_ready, 1)
                    gp_.wait_ge(xve_ready, s + 4)
                    nc.gpsimd.tensor_tensor(x_rstd[:, :], xv_eps[:, :], expo[:, 0, 0:1], ALU.pow).then_inc(xrs_ready, 1)
                if k + 3 == 0:
                    gp_.wait_ge(w_hi_ready, 1)
                    nc.gpsimd.tensor_tensor(w_lo[:, 2, :], w_raw[:, 2, :], w_hi[:, 2, :].bitcast(F32), ALU.subtract).then_inc(wv_ready, 1)
                if has(k + 1):
                    for n in range(2):
                        gp_.wait_ge(ss_ready, 2 * s + (3 + n))
                        nc.gpsimd.tensor_tensor(var_eps[:, n, :], ss[:, n, :], eps[:, n, :], ALU.add).then_inc(ve_ready, 1)
                        gp_.wait_ge(ve_ready, 2 * s + (3 + n))
                        nc.gpsimd.tensor_tensor(rstd[:, n, :], var_eps[:, n, :], expo[:, n, :], ALU.pow).then_inc(rstd_ready, 1)
                if has(k - 2):
                    rstd2(s - 2)
                if has(k):
                    gp_.wait_ge(rinv_ready, s + 1)
                    pv = prob[:, :, :, :].rearrange("p a b n -> p (a b) n")
                    nc.gpsimd.tensor_tensor(pv, pv, rinv[:, :].unsqueeze(2).to_broadcast([P, 2 * PAIRS, S]), ALU.mult).then_inc(p_ready, 1)
                if k in W1_STEPS:
                    gp_.wait_ge(w1hi_ready, s - (STEADY.start - 1))
                    for at in w1_slices(s, k):
                        nc.gpsimd.tensor_tensor(w1_lo_cols[:, at], w1_raw_cols[:, at], w1_hi_cols[:, at].bitcast(F32), ALU.subtract).then_inc(ffw_ready, 1)

            steps(gp_, step)

            nc.gpsimd.tensor_copy(wg_hi[:, :], wg_raw[:, :]).then_inc(ffw_ready, 1)
            gp_.wait_ge(ffw_ready, len(W1_STEPS) + 1)
            nc.gpsimd.tensor_tensor(wg_lo[:, :], wg_raw[:, :], wg_hi[:, :].bitcast(F32), ALU.subtract).then_inc(ffw_ready, 1)

            def group(g, par, last):
                wait_apart(gp_, f_slot, g + 1, (f_row, 3 * g + 3))
                for c in range(2):
                    for j in range(GT):
                        gp_.indirect_dma_start(out=routed[:, :], out_offset=bass.IndirectOffsetOnAxis(ap=slot[:, par, c, j:j + 1], axis=0),
                                               in_=rows[:, par, c, j, :], in_offset=None).then_inc(f_sent[par], 16)

            gp_.wait_ge(y_done, TILES)
            nc.gpsimd.memset(pad[:, :, :], 0.0).then_inc(pad_ready, 1)
            gp_.wait_ge(pad_ready, 1)
            nc.gpsimd.tensor_copy(pad[:, :, D].bitcast(I32), i32s[:, 200:200 + 2 * E]).then_inc(pad_ready, 1)
            n1 = E * FF // P
            gp_.dma_start(b_raw[:, 0:n1], b1.rearrange("e f -> (e f)").rearrange("(p n) -> p n", p=P)).then_inc(bias_in, 16)
            gp_.dma_start(b_raw[:, n1:BC], b2.rearrange("e f -> (e f)").rearrange("(p n) -> p n", p=P)).then_inc(bias_in, 16)
            nc.gpsimd.memset(b1_parts[:, :, :], 0.0).then_inc(bias_prep, 1)
            nc.gpsimd.memset(b2_parts[:, :, :], 0.0).then_inc(bias_prep, 1)
            gp_.wait_ge(bias_in, 32)
            done = 2
            for n in range(3):
                if n > 0:
                    gp_.wait_ge(bias_prep, done)
                    nc.gpsimd.tensor_tensor(b_raw[:, :], b_raw[:, :], b_cols[:, n - 1, :], ALU.subtract).then_inc(bias_prep, 1)
                    done += 1
                    gp_.wait_ge(bias_prep, done)
                nc.gpsimd.tensor_copy(b_cols[:, n, :], b_raw[:, :]).then_inc(bias_prep, 1)
                done += 1
            gp_.wait_ge(bias_prep, done)
            for lo, hi, dram in ((0, n1, bias1), (n1, BC, bias2)):
                gp_.dma_start(dram.rearrange("a (p n) -> p a n", p=P), b_cols[:, :, lo:hi]).then_inc(bias_in, 16)
            gp_.wait_ge(bias_in, 64)
            for n in range(3):
                at = slice(32 * n, 32 * n + 1)
                gp_.dma_start(b1_parts[at, :, :].rearrange("p e n -> p (e n)"), bias1[n:n + 1, :]).then_inc(bias_ready, 16)
                gp_.dma_start(b2_parts[at, :, :].rearrange("p e n -> p (e n)"), bias2[n:n + 1, :]).then_inc(bias_ready, 16)
            groups(gp_, group)

            def row_step(n, q, k, u):
                if is_row_tile(k - 1):
                    b4 = (q - 1) % 4
                    wait_apart(gp_, r_yb, n)
                    gp_.indirect_dma_start(out=results[:, :], out_offset=bass.IndirectOffsetOnAxis(ap=xs_ix[:, b4:b4 + 1], axis=0),
                                           in_=yb[:, b4, :], in_offset=None).then_inc(r_sent[b4], 16)

            row_steps(gp_, row_step)

        @block.vector
        def _(ve):
            def prepare_weights():
                for n in range(2):
                    ve.wait_ge(w_in[n], 16)
                    nc.vector.tensor_reduce(w_mean[:, n, :], w_raw[:, n, :].rearrange("p (h d) -> p h d", h=HEADS), AX.X, ALU.add).then_inc(w_step, 1)
                ve.wait_ge(w_step, 2)
                nc.vector.tensor_scalar(w_mean[:, :, :], w_mean[:, :, :], 1.0 / HD, None, ALU.mult).then_inc(w_step, 1)
                ve.wait_ge(w_step, 3)
                for n in range(2):
                    wv_ = w_raw[:, n, :].rearrange("p (h d) -> p h d", h=HEADS)
                    nc.vector.tensor_tensor(wv_, wv_, w_mean[:, n, :].unsqueeze(2).to_broadcast([P, HEADS, HD]), ALU.subtract).then_inc(w_centred, 1)
                for n in range(2):
                    ve.wait_ge(w_hi_ready, n + 2)
                    ve.wait_ge(w_centred, n + 1)
                    nc.vector.tensor_tensor(w_lo[:, n, :], w_raw[:, n, :], w_hi[:, n, :].bitcast(F32), ALU.subtract).then_inc(w_ready, 1)

            def step(s, par, k):
                if has(k + 2):
                    ve.wait_ge(xhi_ready, s + 3)
                    nc.vector.tensor_tensor(xc_lo[:, par, :, :].rearrange("p a n -> p (a n)"), ps[6][:, 0:256],
                                            xc_hi[:, par, :, :].rearrange("p a n -> p (a n)").bitcast(F32), ALU.subtract).then_inc(xlo_ready, 1)
                if has(k):
                    scale_qk(1, 0, s, k - 1)
                if has(k - 2):
                    ve.wait_ge(y_done, s - 1)
                    nc.vector.scalar_tensor_tensor(y_tmp[:, :], ps[7][:, 0:D], tg[:, 0:1], tgbu[:, :], ALU.mult, ALU.add).then_inc(y_read, 1)
                if has(k):
                    scale_qk(1, 1, s, k - 1)
                if has(k + 3):
                    if k + 3 == 0:
                        ve.wait_ge(x_first, 16)
                    if k + 3 == TILES // 8:
                        ve.wait_ge(x_in, 16)
                    if k + 3 >= 1:
                        ve.wait_ge(xn_ready, s + 3)
                    nc.vector.bn_stats(bn6[:, :], tile_of(x_res, s + 3)).then_inc(bn_done, 1)
                    wait_apart(ve, bn_done, s + 4)
                    nc.vector.bn_aggr(mv[:, :], bn6[:, :]).then_inc(mv_ready, 1)
                if has(k - 2):
                    xs = tile_of(x_res, s - 2)
                    ve.wait_ge(y_read, s - 1)
                    nc.vector.tensor_tensor(xs, xs, y_tmp[:, :], ALU.add).then_inc(x1_ready, 1)
                    wait_apart(ve, x1_ready, s - 1)
                    nc.vector.bn_stats(bn6_2[:, :], xs).then_inc(bn2_done, 1)
                    wait_apart(ve, bn2_done, s - 1, *([(mv2_ready, s - 2)] if k >= 3 else []))
                    nc.vector.bn_aggr(mv_tile[:, :], bn6_2[:, :]).then_inc(agg2_done, 1)
                    ve.wait_ge(agg2_done, s - 1)
                    nc.vector.tensor_copy(tile_of(mv_2, s - 2), mv_tile[:, :]).then_inc(mv2_ready, 1)
                if has(k + 3):
                    ve.wait_ge(xrs_ready, s + 4)
                    if k + 3 >= 1:
                        ve.wait_ge(xt_done, s + 3)
                    nc.vector.tensor_scalar(xn[:, :], tile_of(x_res, s + 3), mv[:, 0:1], x_rstd[:, 0:1], ALU.subtract, ALU.mult).then_inc(xn_ready, 1)
                    if k + 3 == 0:
                        prepare_weights()
                    if k + 3 == 4:
                        ve.wait_ge(tanh_ready, 1)
                        nc.vector.tensor_scalar(tgbu[:, :], bu_b[:, :], tg[:, 0:1], None, ALU.mult).then_inc(tgbu_ready, 1)
                        ve.wait_ge(tgbu_ready, 1)
                def sum_squares(n):
                    ve.wait_ge(sq_ready, 4 * s + (6 + 2 * n))
                    if k + 1 >= 1:
                        ve.wait_ge(ve_ready, 2 * s + (1 + n))
                    nc.vector.tensor_reduce(ss[:, n, :], sq[:, n, :].rearrange("p (h d) -> p h d", h=HEADS), AX.X, ALU.add).then_inc(ss_ready, 1)

                if has(k + 1):
                    sum_squares(0)
                if has(k):
                    for j in range(2):
                        ve.wait_ge(s_done, 2 * s + (j + 1))
                        sv = ps[4 + j][:, :].rearrange("p (a n) -> p a n", a=PAIRS)
                        nc.vector.tensor_reduce(mx[:, j, :], sv, AX.X, ALU.max).then_inc(mx_ready, 1)
                        if k >= 1 and j == 0:
                            ve.wait_ge(pt_done, 2 * s)
                        ve.wait_ge(mx_ready, 2 * s + (j + 1))
                        nc.vector.tensor_tensor(prob[:, :, j, :], sv, mx[:, j, :].unsqueeze(2).to_broadcast([P, PAIRS, S]),
                                                ALU.subtract).then_inc(sub_ready, 1)
                if has(k + 1):
                    sum_squares(1)
                    for half in range(2):
                        scale_qk(0, half, s + 1, k)
                if has(k):
                    ve.wait_ge(exp_ready, s + 1)
                    nc.vector.tensor_reduce(sm[:, :], prob[:, :, :, :].rearrange("p a b n -> p (a b) n"), AX.X, ALU.add).then_inc(sum_ready, 1)
                    ve.wait_ge(sum_ready, s + 1)
                    if k >= 1:
                        ve.wait_ge(p_ready, s)
                    nc.vector.reciprocal(rinv[:, :], sm[:, :]).then_inc(rinv_ready, 1)

            def scale_qk(n, half, t, before_):
                if half == 0:
                    ve.wait_ge(rstd_ready, 2 * t + (1 + n))
                    if before_ >= 0:
                        ve.wait_ge(kt_done if n else qt_done, 2 * t)
                nc.vector.tensor_tensor(
                    qk_n[:, n, half * 512:(half + 1) * 512].rearrange("p (h d) -> p h d", h=8),
                    ps[2 * n + half][:, :].rearrange("p (h d) -> p h d", h=8),
                    rstd[:, n, half * 8:half * 8 + 8].unsqueeze(2).to_broadcast([P, 8, HD]), ALU.mult).then_inc(qn_ready, 1)

            steps(ve, step)

            def normalise(g, par):
                for j in range(GT):
                    t = GT * g + j
                    nc.vector.tensor_scalar(normed[:, par, j, :], tile_of(x_res, t), tile_of(mv_2, t)[:, 0:1], col_of(rstd_2, t),
                                            ALU.subtract, ALU.mult).then_inc(f_xn, 1)

            ve.wait_ge(kt_done, 2 * TILES)
            ve.wait_ge(rstd2_ready, 2 * GT)
            normalise(0, 0)
            normalise(1, 1)
            ve.wait_ge(x1_ready, TILES)
            nc.vector.tensor_scalar(tg01[:, :], tg[:, 1:2], SHARED, None, ALU.mult).then_inc(run0, 1)
            nc.vector.memset(run[:, 0, :], 0.0).then_inc(run0, 1)
            nc.vector.memset(rows3[:, :], 0.0).then_inc(run0, 1)
            ve.wait_ge(run0, 3)
            for n in range(3):
                nc.vector.memset(rows3[32 * n:32 * n + 1, :], 1.0).then_inc(rows3_ready, 1)
            nc.vector.tensor_scalar(tgbs2[:, :], tgbs2[:, :], tg01[:, 0:1], None, ALU.mult).then_inc(run0, 1)
            ve.wait_ge(run0, 4)
            ve.wait_ge(gp_const, 5)

            def shared_out(g):
                ve.wait_ge(fy_done, g + 1)
                xg = x_res[:, GT * g:GT * g + GT, :] if isinstance(g, int) else x_res[:, bass.ds(GT * g, GT), :]
                xg = xg.rearrange("p j d -> p (j d)")
                nc.vector.scalar_tensor_tensor(y8, ps[4][:, :], tg01[:, 0:1], xg, ALU.mult, ALU.add).then_inc(f_x2, 1)
                ve.wait_ge(f_x2, 2 * g + 1)
                nc.vector.tensor_tensor(xg.rearrange("p (j d) -> p j d", j=GT), y8.rearrange("p (j d) -> p j d", j=GT),
                                        tgbs2[:, :].unsqueeze(1).to_broadcast([P, GT, D]), ALU.add).then_inc(f_x2, 1)

            def lo_part(g):
                ve.wait_ge(f_hi, g + 1)
                nc.vector.tensor_tensor(gT_lo, ps[6][:, :], gT_hi.bitcast(F32), ALU.subtract).then_inc(f_lo, 1)

            def less_maximum(g):
                ve.wait_ge(f_lg, g + 1)
                lg = ps[7][:, 0:GT * E].rearrange("p (j e) -> p j e", j=GT)
                nc.vector.tensor_reduce(gm, lg, AX.X, ALU.max).then_inc(f_dve, 1)
                ve.wait_ge(f_dve, 15 * g + 1)
                nc.vector.tensor_tensor(gp, lg, gm.unsqueeze(2).to_broadcast([P, GT, E]), ALU.subtract).then_inc(f_dve, 1)

            def group(g, par, last):
                ve.wait_ge(f_exp, g + 1)
                nc.vector.tensor_reduce(gs, gp, AX.X, ALU.add).then_inc(f_dve, 1)
                ve.wait_ge(f_dve, 15 * g + 3)
                nc.vector.reciprocal(gs, gs).then_inc(f_dve, 1)
                ve.wait_ge(f_dve, 15 * g + 4)
                nc.vector.tensor_tensor(gp, gp, gs.unsqueeze(2).to_broadcast([P, GT, E]), ALU.mult).then_inc(f_dve, 1)
                wait_apart(ve, f_dve, 15 * g + 5)
                for j in range(GT):
                    nc.vector.max(gtop[:, j, :], gp[:, j, :]).then_inc(f_ab, 1)
                wait_apart(ve, f_ab, 2 * GT * g + GT)
                for j in range(GT):
                    nc.vector.max_index(gidx[:, j, :], gtop[:, j, :], gp[:, j, :]).then_inc(f_ab, 1)
                nc.vector.tensor_reduce(gs, gtop[:, :, 0:2], AX.X, ALU.add).then_inc(f_dve, 1)
                ve.wait_ge(f_dve, 15 * g + 6)
                nc.vector.tensor_scalar(gs, gs, TOPK_EPS, None, ALU.add).then_inc(f_dve, 1)
                ve.wait_ge(f_dve, 15 * g + 7)
                nc.vector.reciprocal(gs, gs).then_inc(f_dve, 1)
                ve.wait_ge(f_dve, 15 * g + 8)
                nc.vector.tensor_tensor(gw, gtop[:, :, 0:2], gs.unsqueeze(2).to_broadcast([P, GT, 2]), ALU.mult).then_inc(f_dve, 1)
                ve.wait_ge(f_ab, 2 * GT * g + 2 * GT)
                nc.vector.tensor_copy(gidf, gidx[:, :, 0:2]).then_inc(f_dve, 1)
                ve.wait_ge(f_dve, 15 * g + 10)
                wt = wtok[:, GT * g:GT * g + GT, :] if isinstance(g, int) else wtok[:, bass.ds(GT * g, GT), :]
                nc.vector.tensor_scalar(wt, gw, tg[:, 1:2], None, ALU.mult).then_inc(f_hot, 1)
                for c in range(2):
                    nc.vector.tensor_tensor(oh[:, c, :, :], iot[:, :].unsqueeze(1).to_broadcast([P, GT, E]),
                                            gidf[:, :, c].unsqueeze(2).to_broadcast([P, GT, E]), ALU.is_equal).then_inc(f_hot, 1)
                ve.wait_ge(f_hot, 3 * g + 3)
                nc.vector.tensor_tensor(chosen[:, 0, :, :], oh[:, 0, :, :], oh[:, 1, :, :], ALU.add).then_inc(f_dve, 1)
                ve.wait_ge(f_dve, 15 * g + 11)
                nc.vector.tensor_copy(chosen[:, 1, 1, :], chosen[:, 0, 0, :]).then_inc(f_dve, 1)
                for j in range(2, GT + 1):
                    ve.wait_ge(f_dve, 15 * g + (10 + j))
                    nc.vector.tensor_tensor(chosen[:, 1, j, :] if j < GT else total[:, :], chosen[:, 1, j - 1, :], chosen[:, 0, j - 1, :],
                                            ALU.add).then_inc(f_dve, 1)
                if not last:
                    lo_part(g + 1)
                ve.wait_ge(f_xn, GT * g + GT)
                if not (isinstance(g, int) and g < 2):
                    ve.wait_ge(f_sent[par], GT * 16 * (g - par))
                for c in range(2):
                    nc.vector.tensor_copy(rows[:, par, c, :, 0:D], normed[:, par, :, :]).then_inc(f_row, 1)
                dest = tok_i[:, :, GT * g:GT * g + GT] if isinstance(g, int) else tok_i[:, :, bass.ds(GT * g, GT)]
                nc.vector.tensor_copy(rows[:, par, :, :, D].bitcast(I32), dest).then_inc(f_row, 1)
                if not (isinstance(g, int) and g + 2 >= GROUPS):
                    ve.wait_ge(f_row, 3 * g + 3)
                    normalise(g + 2, par)
                if not last:
                    shared_out(g)
                    less_maximum(g + 1)
                ve.wait_ge(f_rank, g + 1)
                rk = ps[5][:, 0:GT * E].rearrange("p (j e) -> p j e", j=GT)
                nc.vector.tensor_tensor(rank, rk, run[:, par, :].unsqueeze(1).to_broadcast([P, GT, E]), ALU.add).then_inc(f_c, 1)
                nc.vector.tensor_tensor(run[:, 1 - par, :], ps[5][:, 256:256 + E], run[:, par, :], ALU.add).then_inc(f_c, 1)
                ve.wait_ge(f_c, 6 * g + 2)
                nc.vector.tensor_tensor(rank, rank, ebase[:, :].unsqueeze(1).to_broadcast([P, GT, E]), ALU.add).then_inc(f_c, 1)
                ve.wait_ge(f_c, 6 * g + 3)
                for c in range(2):
                    nc.vector.tensor_tensor(hit[:, c, :, :], oh[:, c, :, :], rank, ALU.mult).then_inc(f_c, 1)
                ve.wait_ge(f_c, 6 * g + 5)
                nc.vector.tensor_reduce(slotf, hit, AX.X, ALU.add).then_inc(f_c, 1)
                ve.wait_ge(f_c, 6 * g + 6)
                nc.vector.tensor_copy(slot[:, par, :, :], slotf).then_inc(f_slot, 1)

            lo_part(0)
            less_maximum(0)
            ve.wait_ge(rstd2_ready, TILES)
            groups(ve, group)
            ve.wait_ge(f_c, 6 * GROUPS)

            chain = [0]

            def link(ins):
                chain[0] += 1
                ins.then_inc(sc_step, 1)
                ve.wait_ge(sc_step, chain[0])

            cnt = run[:, GROUPS % 2, :]
            nc.vector.tensor_copy(cnt_i[:, :], cnt).then_inc(cnt_ready, 1)
            link(nc.vector.tensor_tensor(big[:, 1:E, :], big[:, 0, :].unsqueeze(1).to_broadcast([P, E - 1, 32]),
                                         cnt[:, 1:E].unsqueeze(2).to_broadcast([P, E - 1, 32]), ALU.is_lt))
            link(nc.vector.tensor_scalar(big[:, 0, :], big[:, 0, :], cnt[:, 0:1], None, ALU.is_lt))
            link(nc.vector.tensor_reduce(nt[:, :], big[:, :, :], AX.X, ALU.add))
            link(nc.vector.tensor_copy(cum[:, 0, :], nt[:, :]))
            src = 0
            for sh in (1, 2, 4):
                link(nc.vector.tensor_copy(cum[:, 1 - src, 0:sh], cum[:, src, 0:sh]))
                link(nc.vector.tensor_tensor(cum[:, 1 - src, sh:E], cum[:, src, sh:E], cum[:, src, 0:E - sh], ALU.add))
                src = 1 - src
            link(nc.vector.tensor_tensor(past[:, :, :], tile_n[:, :].unsqueeze(2).to_broadcast([P, NT, E]),
                                         cum[:, src, :].unsqueeze(1).to_broadcast([P, NT, E]), ALU.is_ge))
            link(nc.vector.tensor_reduce(sched[:, 0, :], past[:, :, :], AX.X, ALU.add))
            link(nc.vector.tensor_tensor(past[:, :, :], past[:, :, :], nt[:, :].unsqueeze(1).to_broadcast([P, NT, E]), ALU.mult))
            link(nc.vector.tensor_reduce(sched[:, 1, :], past[:, :, :], AX.X, ALU.add))
            link(nc.vector.tensor_tensor(sched[:, 1, :], tile_n[:, :], sched[:, 1, :], ALU.subtract))
            link(nc.vector.tensor_scalar(sched[:, 2, :], sched[:, 0, :], float(REGION), None, ALU.mult))
            link(nc.vector.tensor_scalar(sched[:, 1, :], sched[:, 1, :], float(P), None, ALU.mult))
            link(nc.vector.tensor_tensor(sched[:, 1, :], sched[:, 1, :], sched[:, 2, :], ALU.add))
            link(nc.vector.tensor_scalar(sched[:, 0, :], sched[:, 0, :], float(E - 1), None, ALU.min))
            nc.vector.tensor_copy(sched_i[:, :, :], sched[:, 0:2, :]).then_inc(sched_ready, 1)
            shared_out(GROUPS - 1)

            def row_step(n, q, k, u):
                par = q % 2
                if is_row_tile(k + 1):
                    b4 = (q + 1) % 4
                    ve.wait_ge(r_in[b4], 4 * (n + (1 - b4)) + 16)
                    if k + 1 >= 4:
                        ve.wait_ge(r_sent[b4], 4 * (n + (1 - b4)))
                    nc.vector.tensor_copy(xs_ix[:, b4:b4 + 1], xs_in[:, b4, D:ROW].bitcast(I32)).then_inc(r_ix, 1)
                if is_row_tile(k + 2):
                    ve.wait_ge(r_hi, n + 3)
                    nc.vector.tensor_tensor(xs_lo[:, par, :], ps[6 + par][:, 0:P], xs_hi[:, par, :].bitcast(F32), ALU.subtract).then_inc(r_lo, 1)
                if is_row_tile(k):
                    if k >= 2:
                        ve.wait_ge(r_y, n - 1)
                    ve.wait_ge(r_ta, n + 1)
                    nc.vector.tensor_copy(hid_T[:, par, :], ps[2 + par][:, :]).then_inc(r_aT, 1)

            row_steps(ve, row_step)

            for g in range(GROUPS):
                ve.wait_ge(o_in[g], 32)
                for j in range(GT):
                    t = GT * g + j
                    nc.vector.scalar_tensor_tensor(x_res[:, t, :], y_in[g][:, 0, j, :], wtok[:, t, 0:1], x_res[:, t, :],
                                                   ALU.mult, ALU.add).then_inc(o_a, 1)
                ve.wait_ge(o_a, GT * g + GT)
                ve.wait_ge(o_w, GT * g + GT)
                nc.vector.tensor_tensor(x_res[:, GT * g:GT * g + GT, :], x_res[:, GT * g:GT * g + GT, :], y_in[g][:, 1, :, :],
                                        ALU.add).then_inc(o_b, 1)

        @block.tensor
        def _(pe):
            pe.wait_ge(ident_ready, 1)
            def project(out_bank, par, src, w, cols):
                nc.tensor.matmul(out_bank, xc_hi[:, par, src, :], w_hi[:, w, cols], start=True, stop=False)
                nc.tensor.matmul(out_bank, xc_hi[:, par, src, :], w_lo[:, w, cols], start=False, stop=False)
                return nc.tensor.matmul(out_bank, xc_lo[:, par, src, :], w_hi[:, w, cols], start=False, stop=True)

            def step(s, par, k):
                cols = (slice(0, 512), slice(512, 1024))

                def transpose_qk(n, done, halves):
                    for j in halves:
                        if n == 1:
                            pe.wait_ge(qT_ready, 2 * s + (j + 1))
                        elif j == 0 and has(k + 2):
                            pe.wait_ge(xlo_ready, s + 3)
                        elif j == 1 and has(k - 2):
                            pe.wait_ge(y_read, s - 1)
                        for a in range(4):
                            c0 = (4 * j + a) * P
                            last = nc.tensor.transpose(ps[6 + j][:, a * P:(a + 1) * P], qk_n[:, n, c0:c0 + P], ident[:, :])
                        last.then_inc(done, 1)

                def project_v(j):
                    if not has(k):
                        pe.wait_ge(wv_ready, 1)
                    if has(k):
                        pe.wait_ge(sub_ready, 2 * s + (j + 1))
                    project(ps[4 + j][:, :], 1 - par, 1, 2, cols[j]).then_inc(v_done, 1)

                if has(k - 2):
                    pe.wait_ge(o_ready, 2 * s - 3)
                if has(k + 2):
                    pe.wait_ge(xn_ready, s + 3)
                    pe.wait_ge(c_loaded[par], 8 * (s + 2 - par) + 16)
                    if k == 1:
                        pe.wait_ge(kT_ready, 2 * s)
                    elif k < 1 and has(k + 1):
                        pe.wait_ge(xlo_ready, s + 2)
                    nc.tensor.transpose(ps[6][:, 0:P], xn[:, :], ident[:, :])
                    nc.tensor.transpose(ps[6][:, P:2 * P], c_in[:, par, :], ident[:, :]).then_inc(xt_done, 1)
                if has(k - 2):
                    if k == 2:
                        pe.wait_ge(wu_in, 16)
                    pe.wait_ge(o_ready, 2 * s - 2)
                    for p in range(PAIRS):
                        last = nc.tensor.matmul(ps[7][:, 0:D], o_T[:, p, :, :].rearrange("p b n -> p (b n)"), wu_sb[:, p, :],
                                                start=(p == 0), stop=(p == PAIRS - 1))
                    last.then_inc(y_done, 1)
                if has(k):
                    pe.wait_ge(qn_ready, 4 * s + 2)
                    transpose_qk(0, qt_done, (0,))
                if has(k + 1):
                    if not has(k):
                        pe.wait_ge(w_ready, 2)
                        pe.wait_ge(xlo_ready, s + 2)
                    project(ps[0][:, :], 1 - par, 0, 0, cols[0]).then_inc(proj_done, 1)
                if has(k):
                    transpose_qk(0, qt_done, (1,))
                if has(k + 1):
                    project(ps[1][:, :], 1 - par, 0, 0, cols[1]).then_inc(proj_done, 1)
                if has(k):
                    pe.wait_ge(qn_ready, 4 * s + 4)
                    transpose_qk(1, kt_done, (0, 1))
                if has(k + 1):
                    for j in range(2):
                        project(ps[2 + j][:, :], 1 - par, 1, 1, cols[j]).then_inc(proj_done, 1)
                def transpose_probabilities(j):
                    if j == 0:
                        pe.wait_ge(p_ready, s)
                        if not has(k) and has(k - 2):
                            pe.wait_ge(y_read, s - 1)
                    if has(k):
                        pe.wait_ge(kT_ready, 2 * s + (j + 1))
                    for a in range(4):
                        last = nc.tensor.transpose(ps[6 + j][:, a * P:(a + 1) * P],
                                                   prob[:, 4 * j + a, :, :].rearrange("p b n -> p (b n)"), ident[:, :])
                    last.then_inc(pt_done, 1)

                for b in range(2):
                    if has(k - 1):
                        transpose_probabilities(b)
                    if has(k):
                        if b == 0:
                            wait_apart(pe, kT_ready, 2 * s + 2)
                        wait_apart(pe, v_ready, 2 * s + (b + 1))
                        for p in range(PAIRS):
                            for h in range(2):
                                rows = slice(h * HD, (h + 1) * HD)
                                last = nc.tensor.matmul(ps[4 + b][rows, p * S:(p + 1) * S], qk_T[rows, 0, p, b * S:(b + 1) * S],
                                                        qk_T[rows, 1, p, b * S:(b + 1) * S], start=True, stop=True)
                        last.then_inc(s_done, 1)
                if has(k + 1):
                    project_v(0)
                for b in range(2):
                    if has(k - 1):
                        if b == 0:
                            wait_apart(pe, pt_ready, 2 * s)
                        rows = slice(b * S, (b + 1) * S)
                        for p in range(PAIRS):
                            for h in range(2):
                                last = nc.tensor.matmul(ps[6 + b][h * HD:(h + 1) * HD, p * S:(p + 1) * S],
                                                        v_sb[rows, 1 - par, (2 * p + h) * HD:(2 * p + h + 1) * HD],
                                                        prob_T[rows, p, h * S:(h + 1) * S], start=True, stop=True)
                        last.then_inc(o_done, 1)
                if has(k + 1):
                    project_v(1)
            steps(pe, step)

            def transpose_tokens(g, par):
                pe.wait_ge(f_xn, GT * g + GT)
                for j in range(GT):
                    last_ = nc.tensor.transpose(ps[6][:, j * P:(j + 1) * P], normed[:, par, j, :], ident[:, :])
                last_.then_inc(f_t, 1)

            def logits(g):
                pe.wait_ge(f_lo, g + 1)
                for j in range(GT):
                    for n, (a, w) in enumerate(((gT_lo, wg_lo), (gT_lo, wg_hi), (gT_hi, wg_lo), (gT_hi, wg_hi))):
                        last_ = nc.tensor.matmul(ps[7][:, j * E:(j + 1) * E], a[:, j * P:(j + 1) * P], w[:, :], start=(n == 0), stop=(n == 3))
                last_.then_inc(f_lg, 1)

            def group(g, par, last):
                for c in range(CH):
                    fs = slice(c * P, (c + 1) * P)
                    nc.tensor.matmul(ps[c][:, :], w1_hi[:, E, fs], gT_hi, start=True, stop=False)
                    nc.tensor.matmul(ps[c][:, :], w1_hi[:, E, fs], gT_lo, start=False, stop=False)
                    nc.tensor.matmul(ps[c][:, :], w1_lo[:, E, fs], gT_hi, start=False, stop=True).then_inc(h_done, 1)
                if not last:
                    transpose_tokens(g + 1, 1 - par)
                if not (isinstance(g, int) and g == 0):
                    pe.wait_ge(f_x2, 2 * g - 1)
                for c in range(CH):
                    pe.wait_ge(act_ready, CH * g + (c + 1))
                for j in range(GT):
                    for c in range(CH):
                        last_ = nc.tensor.matmul(ps[4][:, j * D:(j + 1) * D], act[:, c, j * P:(j + 1) * P], w2_sb[:, E, c, :],
                                                 start=(c == 0), stop=(c == CH - 1))
                last_.then_inc(fy_done, 1)
                if not last:
                    logits(g + 1)
                pe.wait_ge(f_dve, 15 * g + 15)
                for j in range(GT):
                    out_j = ps[5][:, j * E:(j + 1) * E]
                    nc.tensor.matmul(out_j, before[:, :], chosen[:, 0, j, :], start=True, stop=(j == 0))
                    if j > 0:
                        nc.tensor.matmul(out_j, ones_b[:, :], chosen[:, 1, j, :], start=False, stop=True)
                nc.tensor.matmul(ps[5][:, 256:256 + E], ones_b[:, :], total[:, :], start=True, stop=True).then_inc(f_rank, 1)

            transpose_tokens(0, 0)
            pe.wait_ge(ffw_ready, len(W1_STEPS) + 2)
            pe.wait_ge(w2_in, 3 * 16)
            pe.wait_ge(y_read, TILES)
            logits(0)
            groups(pe, group)
            pe.wait_ge(sched_ready, 1)
            pe.wait_ge(bias_ready, 96)
            pe.wait_ge(rows3_ready, 3)

            expert = {}

            def row_step(n, q, k, u):
                par = q % 2
                if is_row_tile(k + 1):
                    e_in = pe.value_load(tile_of_sched(0, n + 1), min_val=0, max_val=E - 1)
                    expert[u + 1] = e_in
                if is_row_tile(k - 1):
                    e_out = expert[u - 1] if u >= 2 else None
                    if e_out is None:
                        e_out = pe.value_load(tile_of_sched(0, n - 1), min_val=0, max_val=E - 1)
                if is_row_tile(k):
                    pe.wait_ge(r_act, n + 1)
                if is_row_tile(k + 1):
                    pe.wait_ge(r_lo, n + 2)
                    h = ps[1 - par][:, :]

                    def of(w):
                        return w[:, bass.ds(e_in, 1), :].rearrange("p a n -> p (a n)")

                    nc.tensor.matmul(h, rows3[:, :], of(b1_parts), start=True, stop=False)
                    nc.tensor.matmul(h, xs_hi[:, 1 - par, :], of(w1_hi), start=False, stop=False)
                    nc.tensor.matmul(h, xs_hi[:, 1 - par, :], of(w1_lo), start=False, stop=False)
                    nc.tensor.matmul(h, xs_lo[:, 1 - par, :], of(w1_hi), start=False, stop=True).then_inc(r_h, 1)
                if is_row_tile(k + 2):
                    b4 = (q + 2) % 4
                    pe.wait_ge(r_in[b4], 4 * (n + (2 - b4)) + 16)
                    nc.tensor.transpose(ps[6 + par][:, 0:P], xs_in[:, b4, 0:D], ident[:, :]).then_inc(r_t, 1)
                if is_row_tile(k - 1):
                    pe.wait_ge(r_aT, n)
                    if not is_row_tile(k):
                        pe.wait_ge(r_yb, n - 2)
                    y = ps[4 + (1 - par)][:, 0:D]
                    nc.tensor.matmul(y, rows3[:, :], b2_parts[:, bass.ds(e_out, 1), :].rearrange("p a n -> p (a n)"), start=True, stop=False)
                    w2e = w2_sb[:, bass.ds(e_out, 1), :, :].rearrange("p a c n -> p (a c) n")
                    for c in range(CH):
                        last_ = nc.tensor.matmul(y, hid_T[:, 1 - par, c * P:(c + 1) * P], w2e[:, c, :], start=False, stop=(c == CH - 1))
                    last_.then_inc(r_y, 1)
                if is_row_tile(k):
                    for c in range(CH):
                        last_ = nc.tensor.transpose(ps[2 + par][:, c * P:(c + 1) * P], hid[:, par, c * P:(c + 1) * P], ident[:, :])
                    last_.then_inc(r_ta, 1)

            row_steps(pe, row_step)


_INS = ['x', 'ctx_1024', 'g_xattn', 'g_ffn', 'L0_xattn_Wq', 'L0_xattn_Wk', 'L0_xattn_Wv', 'L0_xattn_Wu', 'L0_xattn_bu',
        'L0_xattn_qn_w', 'L0_xattn_qn_b', 'L0_xattn_kn_w', 'L0_xattn_kn_b', 'L0_ffn_Wg', 'L0_ffn_W1', 'L0_ffn_b1',
        'L0_ffn_W2', 'L0_ffn_b2', 'L0_ffn_Ws1', 'L0_ffn_bs1', 'L0_ffn_Ws2', 'L0_ffn_bs2']
_TRANSPOSED = ('L0_xattn_Wq', 'L0_xattn_Wk', 'L0_xattn_Wv', 'L0_xattn_Wu')
_BY_HIDDEN_UNIT = ('L0_ffn_bs1',)


def kernel(**inputs):
    import numpy as np
    import concourse.bacc as bacc
    from concourse.bass_utils import run_bass_kernel_spmd

    nc = bacc.Bacc("TRN2", target_bir_lowering=False, num_devices=1)
    arrays, args = {}, []
    for name in _INS:
        a = np.asarray(inputs[name])
        if name in _TRANSPOSED:
            a = a.T
        if name in _BY_HIDDEN_UNIT:
            a = a.reshape(-1, P).T
        a = np.ascontiguousarray(a)
        arrays[f"in_{name}"] = a
        args.append(nc.dram_tensor(f"in_{name}", a.shape, mybir.dt.from_np(a.dtype), kind="ExternalInput").ap())
    args.append(nc.dram_tensor("out_x", [B, S, D], F32, kind="ExternalOutput").ap())
    flamingo_block(nc, *args)
    r = run_bass_kernel_spmd(nc, [arrays], core_ids=[0])
    return r.results[0]["out_x"]
```
